# Optimizing a Trainium2 kernel written in Bass

```python
import numpy as np
import jax
import jax.numpy as jnp

def _softmax(x, axis=-1):
    return jax.nn.softmax(x, axis=axis)

def _gelu(x):
    return jax.nn.gelu(x, approximate=True)

def _silu(x):
    return jax.nn.silu(x)

def _sigmoid(x):
    return jax.nn.sigmoid(x)

def _layernorm(x, axis=-1, eps=1e-05):
    m = jnp.mean(x, axis=axis, keepdims=True)
    v = jnp.var(x, axis=axis, keepdims=True)
    return (x - m) / jnp.sqrt(v + eps)

def _scatter_add(tgt, idx, src, axis=0):
    return tgt.at[idx].add(src)

def _segment_sum(src, seg, n):
    return jax.ops.segment_sum(src, seg, n)
kernel_name = 'mk_seq_preln_d1_jaxref_r4_45ac32'

def setup_inputs(seed: int=0):
    np.random.seed(seed)
    _w = jnp.asarray

    def _L0_attn_setup():
        import jax, jax.numpy as jnp
        import numpy as np
        B, T, D, N = (2, 512, 256, 16)
        DT_RANK = 64

        def _selective_scan(A_bar, B_bar, C):

            def step(h, inputs):
                a_t, b_t, c_t = inputs
                h = a_t * h + b_t
                y_t = jnp.einsum('bdn,bn->bd', h, c_t)
                return (h, y_t)
            h0 = jnp.zeros(A_bar.shape[:1] + A_bar.shape[2:], dtype=A_bar.dtype)
            xs = (jnp.moveaxis(A_bar, 1, 0), jnp.moveaxis(B_bar, 1, 0), jnp.moveaxis(C, 1, 0))
            _, ys = jax.lax.scan(step, h0, xs)
            return jnp.moveaxis(ys, 0, 1)
        key = jax.random.key(seed)
        ks = jax.random.split(key, 8)
        x = jax.random.normal(ks[0], (B, T, D), dtype=jnp.float32)
        W_B = jax.random.normal(ks[1], (N, D), dtype=jnp.float32) / np.sqrt(D)
        W_C = jax.random.normal(ks[2], (N, D), dtype=jnp.float32) / np.sqrt(D)
        W_dt1 = jax.random.normal(ks[3], (DT_RANK, D), dtype=jnp.float32) / np.sqrt(D)
        W_dt2 = jax.random.normal(ks[4], (D, DT_RANK), dtype=jnp.float32) / np.sqrt(DT_RANK)
        dt_min, dt_max = (0.001, 0.1)
        u = jax.random.uniform(ks[5], (D,), dtype=jnp.float32)
        dt_init = jnp.clip(jnp.exp(u * (np.log(dt_max) - np.log(dt_min)) + np.log(dt_min)), 0.0001, None)
        b_dt2 = dt_init + jnp.log(-jnp.expm1(-dt_init))
        a = jax.random.uniform(ks[6], (N,), dtype=jnp.float32) * 0.5 + 0.5
        log_A = jnp.broadcast_to(jnp.log(a)[None, :], (D, N)).copy()
        D_skip = jnp.ones((D,), dtype=jnp.float32)
        return {'x': x, 'W_B': W_B, 'W_C': W_C, 'W_dt1': W_dt1, 'W_dt2': W_dt2, 'b_dt2': b_dt2, 'log_A': log_A, 'D_skip': D_skip}
    _L0_attn_in = _L0_attn_setup()

    def _L0_ffn_setup():
        import jax, jax.numpy as jnp
        import numpy as np
        B, S, D, E, H = (4, 512, 256, 8, 1024)
        key = jax.random.key(seed)
        ks = jax.random.split(key, 7)
        scale_d = 1.0 / np.sqrt(D)
        scale_h = 1.0 / np.sqrt(H)
        return {'x': jax.random.normal(ks[0], (B, S, D), dtype=jnp.float32), 'Wr': jax.random.uniform(ks[1], (D, E), jnp.float32, -scale_d, scale_d), 'br': jnp.zeros((E,), jnp.float32), 'W1': jax.random.uniform(ks[2], (E, D, H), jnp.float32, -scale_d, scale_d), 'b1': jax.random.uniform(ks[3], (E, H), jnp.float32, -scale_d, scale_d), 'W2': jax.random.uniform(ks[4], (E, H, D), jnp.float32, -scale_h, scale_h), 'b2': jax.random.uniform(ks[5], (E, D), jnp.float32, -scale_h, scale_h)}
    _L0_ffn_in = _L0_ffn_setup()
    _d = {'L0_attn_x': _L0_attn_in['x'], 'L0_attn_W_B': _L0_attn_in['W_B'], 'L0_attn_W_C': _L0_attn_in['W_C'], 'L0_attn_W_dt1': _L0_attn_in['W_dt1'], 'L0_attn_W_dt2': _L0_attn_in['W_dt2'], 'L0_attn_b_dt2': _L0_attn_in['b_dt2'], 'L0_attn_log_A': _L0_attn_in['log_A'], 'L0_attn_D_skip': _L0_attn_in['D_skip'], 'L0_ffn_Wr': _L0_ffn_in['Wr'], 'L0_ffn_br': _L0_ffn_in['br'], 'L0_ffn_W1': _L0_ffn_in['W1'], 'L0_ffn_b1': _L0_ffn_in['b1'], 'L0_ffn_W2': _L0_ffn_in['W2'], 'L0_ffn_b2': _L0_ffn_in['b2']}
    _x0 = _d['L0_attn_x']
    _d['L0_attn_x'] = jax.random.normal(jax.random.fold_in(jax.random.key(seed), 1), (2, 2048, 256), dtype=_x0.dtype)
    del _x0
    return _d

def reference(L0_attn_x, L0_attn_W_B, L0_attn_W_C, L0_attn_W_dt1, L0_attn_W_dt2, L0_attn_b_dt2, L0_attn_log_A, L0_attn_D_skip, L0_ffn_Wr, L0_ffn_br, L0_ffn_W1, L0_ffn_b1, L0_ffn_W2, L0_ffn_b2):

    def _L0_attn_ref(x, W_B, W_C, W_dt1, W_dt2, b_dt2, log_A, D_skip):
        import jax, jax.numpy as jnp
        import numpy as np
        B, T, D, N = (2, 512, 256, 16)
        DT_RANK = 64

        def _selective_scan(A_bar, B_bar, C):

            def step(h, inputs):
                a_t, b_t, c_t = inputs
                h = a_t * h + b_t
                y_t = jnp.einsum('bdn,bn->bd', h, c_t)
                return (h, y_t)
            h0 = jnp.zeros(A_bar.shape[:1] + A_bar.shape[2:], dtype=A_bar.dtype)
            xs = (jnp.moveaxis(A_bar, 1, 0), jnp.moveaxis(B_bar, 1, 0), jnp.moveaxis(C, 1, 0))
            _, ys = jax.lax.scan(step, h0, xs)
            return jnp.moveaxis(ys, 0, 1)
        B_t = jnp.einsum('btd,nd->btn', x, W_B)
        C_t = jnp.einsum('btd,nd->btn', x, W_C)
        dt_raw = jnp.einsum('btr,dr->btd', jnp.einsum('btd,rd->btr', x, W_dt1), W_dt2) + b_dt2
        dt = jax.nn.softplus(dt_raw)
        A = -jnp.exp(log_A)
        A_bar = jnp.exp(dt[..., None] * A[None, None])
        dB = (A_bar - 1.0) / (A[None, None] + 1e-08)
        B_bar = dB * x[..., None] * B_t[:, :, None, :]
        y = _selective_scan(A_bar, B_bar, C_t)
        return y + D_skip * x

    def _L0_ffn_ref(x, Wr, br, W1, b1, W2, b2):
        import jax, jax.numpy as jnp
        import numpy as np
        B, S, D, E, H = (4, 512, 256, 8, 1024)
        route_logits = jnp.einsum('bsd,de->bse', x, Wr) + br
        routing_weights = jax.nn.softmax(route_logits, axis=-1)
        selected_expert = jnp.argmax(routing_weights, axis=-1)
        num_experts = W1.shape[0]
        out = jnp.zeros_like(x)
        for e in range(num_experts):
            h = jax.nn.gelu(jnp.einsum('bsd,dh->bsh', x, W1[e]) + b1[e], approximate=False)
            y = jnp.einsum('bsh,hd->bsd', h, W2[e]) + b2[e]
            out = jnp.where((selected_expert == e)[..., None], y, out)
        return out
    x = L0_attn_x
    x = x + _L0_attn_ref(_layernorm(x, axis=-1), L0_attn_W_B, L0_attn_W_C, L0_attn_W_dt1, L0_attn_W_dt2, L0_attn_b_dt2, L0_attn_log_A, L0_attn_D_skip)
    x = x + _L0_ffn_ref(_layernorm(x, axis=-1), L0_ffn_Wr, L0_ffn_br, L0_ffn_W1, L0_ffn_b1, L0_ffn_W2, L0_ffn_b2)
    return x

_drawn_inputs = setup_inputs


def setup_inputs(seed=0):
    import zlib

    import numpy as np

    out = dict(_drawn_inputs(seed))
    spreads = {'L0_attn_D_skip': (1.0, 0.2), 'L0_ffn_br': (0.0, 0.1)}
    factors = {'L0_ffn_b1': 8.0, 'L0_ffn_b2': 6.951}
    for name, (base, spread) in spreads.items():
        noise = np.random.default_rng([zlib.crc32(name.encode()), seed]).standard_normal(out[name].shape)
        drawn = base * np.exp(spread * noise) if base else spread * noise
        out[name] = jnp.asarray(drawn.astype(out[name].dtype))
    for name, factor in factors.items():
        out[name] = (out[name] * factor).astype(out[name].dtype)
    return out
```

```python
from contextlib import ExitStack

import numpy as np

import concourse.bass as bass
from concourse import mybir

F32 = mybir.dt.float32
BF16 = mybir.dt.bfloat16
U32 = mybir.dt.uint32
ALU = mybir.AluOpType
ACT = mybir.ActivationFunctionType
AX = mybir.AxisListType

P = 128
B, T, D = 2, 2048, 256
N = 16
R = 64
E, H = 8, 1024
ROWS = B * T
TC = 512
NC = T // TC
NQ = B * NC
TI = TC // P
KD = D // P
KH = H // P
ITEMS = N * KD
MT = ROWS // P + E - 1
CAP = ROWS // P
FAR = 1.0e6
EPS = 1e-5

SMALL = dict(ident=P, logA=KD * N, bdt2=KD, dskip=KD, wr=KD * E, wbc=KD * 96, wdt1=KD * R, wdt2=D,
             b1=E * KH, tri=P, spread=32, e_less8=E, e_base=E, tok0=B * TI, j128=32, tile_no=MT, br=E)
OFF = {}
_at = 0
for _name, _w in SMALL.items():
    OFF[_name] = (_at, _at + _w)
    _at += _w
SW = _at

POST = {"z01": 1, "z23": 2, "xnr0": 7, "xnr1": 8, "route": 9, "rank": 13}
PRE = {"xn0": 3, "xn1": 4, "bc": 5, "dt1": 6, "dt2_0": 10, "dt2_1": 11}
LAST_BASE = 12 * NQ - 6
RT_STEPS = 16


def hops(first, last):
    names = ({} if first else POST) | ({} if last else PRE)
    order = sorted(names, key=names.get)
    return {names[x]: (x, i) for i, x in enumerate(order)}, {x: i for i, x in enumerate(order)}


def hop_base(q):
    return 6 if isinstance(q, int) and q == 0 else 12 * q


def wait(eng, sem, value):
    if not (isinstance(value, int) and value <= 0):
        eng.wait_ge(sem, value)


def wait_alone(eng, sem, value, met):
    value = value if isinstance(value, int) else eng.to_reg(value)
    eng.wait_ge(met, 1)
    eng.wait_ge(sem, value)


def expert_tiles(eng, step):
    for u in range(3):
        step(u, u, 0)
    with eng.Fori(1, MT // 3 - 1) as r:
        for u in range(3):
            step(3 * r + u, u, r)
    for u in range(3):
        step(MT - 3 + u, u, MT // 3 - 1)


def build(nc, x, small, w1, w2, b2, out):
    with ExitStack() as ctx:
        def sb(name, shape, dt=F32):
            return ctx.enter_context(nc.sbuf_tensor(name, shape, dt))

        def ps(name, shape):
            return ctx.enter_context(nc.psum_tensor(name, shape, F32))

        def sem(name):
            return ctx.enter_context(nc.semaphore(name))

        xrows = x.rearrange("b t d -> (b t) d")
        outrows = out.rearrange("b t d -> (b t) d")
        token_rows = nc.dram_tensor("token_rows", [ROWS, 2 * D], F32, kind="Internal").ap()
        lists = nc.dram_tensor("lists", [E * ROWS, 1], F32, kind="Internal").ap()

        sm = sb("sm", [P, SW])

        def col(name, a=0, b=None):
            lo, hi = OFF[name]
            return sm[:, lo + a:(hi if b is None else lo + b)]

        ident = col("ident")
        w1_sb = sb("w1_sb", [P, KD, E * H])
        w2_sb = sb("w2_sb", [P, E * KH * D])
        b2_sb = sb("b2_sb", [P, E * D])
        negA = sb("negA", [P, KD * N])
        invA = sb("invA", [P, KD * N])
        tri_bf = sb("tri_bf", [P, P], BF16)
        ones_bf = sb("ones_bf", [P, P], BF16)
        sel = sb("sel", [96, 32, P], BF16)

        ring_at = (E // 2) * KH * D

        def ring(i, j):
            a = ring_at + (4 * i + j) * TC
            return w2_sb[:, a:a + TC]

        Bsb = [ring(0, j) for j in range(4)]
        vb = [ring(1, j) for j in range(4)]
        hb = [ring(2, j) for j in range(4)]
        hc = [ring(3, j) for j in range(4)]
        bb = [sb(f"b{i}", [P, TC]) for i in range(2)]
        xin = sb("xin", [P, TI, D])
        xnT = [[sb(f"xnT{b}{h}", [P, TC]) for h in range(KD)] for b in range(B)]
        dts = [sb(f"dt{b}", [P, KD * TC]) for b in range(B)]
        mag = sb("mag", [P, KD * TC])
        bc32 = sb("bc32", [96, TC])
        rest = sb("rest", [96, TC])
        bc3 = [sb(f"bc3_{b}", [96, TC], BF16) for b in range(B)]
        t1 = sb("t1", [R, TC])
        hlast = [sb(f"hlast{b}", [P, ITEMS]) for b in range(B)]
        z = [sb(f"z{h}", [P, TC]) for h in range(KD)]
        row = sb("row", [P, TI, 2 * D])
        xnrT = [sb(f"xnrT{h}", [P, TC]) for h in range(KD)]
        st = [sb(f"st{i}", [P, TI * 6]) for i in range(2)]
        mv = [sb(f"mv{i}", [P, TI, 2]) for i in range(2)]
        ve = [sb(f"ve{i}", [P, TI]) for i in range(2)]
        rs = [sb(f"rs{i}", [P, TI]) for i in range(2)]
        mhalf = sb("mhalf", [P, TI])
        eps = sb("eps", [P, TI])
        zero = sb("zero", [P, 1])
        lg = sb("lg", [P, TI, E])
        red = sb("red", [P, TI])
        pick = sb("pick", [P, TI])
        onehot = sb("onehot", [P, TI, E], BF16)
        run = sb("run", [P, TI + 1, E])
        slot = sb("slot", [P, TI, E])
        slotf = sb("slotf", [P, TI])
        slotu = sb("slotu", [P, TI], U32)
        tokf = sb("tokf", [P, B * TI])

        hsb = dts[0][:, :]
        hT = dts[1][:, :]
        xT = mag[:, 0:D]
        yo = [mag[:, D:2 * D], mag[:, 2 * D:3 * D], mag[:, 3 * D:4 * D]]
        mrow = [row[:, i, :] for i in range(3)]
        b1c = [sb(f"b1c{i}", [P, KH]) for i in range(3)]
        gcol = [sb(f"gcol{i}", [P, 1], U32) for i in range(3)]
        cum = sb("cum", [P, E + 1])
        ntile = sb("ntile", [P, E])
        big = xnT[0][0]
        big2 = xnT[0][1]
        tile_e = sb("tile_e", [P, MT])
        tile_c = sb("tile_c", [P, MT])
        tile_eu = sb("tile_eu", [P, MT], U32)
        tile_cu = sb("tile_cu", [P, MT], U32)
        lists_in = xnT[1][0][:, 0:E * CAP]
        farf = xnT[1][1][:, 0:E * CAP]
        ids = sb("ids", [P, E * CAP + 1], U32)

        bank = [ps(f"bank{i}", [P, 512]) for i in range(3)]
        A = [bank[0], bank[1]]
        Bps = bank[2]
        misc = ps("misc", [P, 512])
        CC = ps("CC", [P, 1024])
        YY = ps("YY", [P, 1024])
        Cps = [CC[:, 0:512], CC[:, 512:1024]]
        Y = [YY[:, 0:512], YY[:, 512:1024]]
        hps = CC[:, :]
        hTps = YY[:, :]
        xTps = bank[0]
        yps = bank[1]

        s_small = sem("small_loaded")
        s_w = sem("w1_loaded")
        s_w2a = sem("w2_lower_loaded")
        s_w2b = sem("w2_upper_loaded")
        s_b2 = sem("b2_loaded")
        s_x = sem("x_loaded")
        s_res = sem("residual_loaded")
        s_const = sem("constants_built")
        s_pconst = sem("gpsimd_constants_built")
        s_Ae = sem("A_exponent")
        s_xn = sem("layernorm1_done")
        s_var = [sem("variance1"), sem("variance2")]
        s_rs = [sem("rstd1"), sem("rstd2")]
        s_ln = sem("layernorm_steps")
        s_full = sem("shared_bank_filled")
        s_free = sem("shared_bank_read")
        s_part = sem("bc_parts_rounded")
        s_rest = sem("bc_parts_left")
        s_pm = sem("softplus_log")
        s_pms = sem("softplus_exp")
        s_dt = sem("dt_ready")
        s_Bps = sem("B_spread")
        s_Bsb = sem("B_copied")
        s_C = sem("C_spread")
        s_a = sem("a_ready")
        s_v = sem("v_ready")
        s_b = sem("b_ready")
        s_h = sem("h_ready")
        s_hl = sem("h_last_kept")
        s_hc = sem("hC_ready")
        s_y = sem("y_added")
        s_z = sem("z_ready")
        s_eps = sem("eps_added")
        s_xn2 = sem("layernorm2_done")
        s_lg = sem("logits_centred")
        s_pe = sem("exponentials")
        s_rt = sem("routing_steps")
        s_oh = sem("onehot_ready")
        s_slot = sem("slots_ready")
        s_far = sem("far_filled")
        s_init = sem("lists_started")
        s_store = sem("token_rows_stored")
        s_scat = sem("tokens_listed")
        s_lists = sem("lists_loaded")
        s_lt = sem("lists_transposed")
        s_tab = sem("table_steps")
        s_table = sem("table_ready")
        s_gcol = sem("gather_index_copied")
        s_row = [sem(f"rows_gathered{i}") for i in range(3)]
        s_b1 = sem("b1_copied")
        s_xTp = sem("xT_transposed")
        s_xT = sem("xT_copied")
        s_hps = sem("hidden_product")
        s_hA = sem("hidden_copied_vector")
        s_hB = sem("hidden_copied_scalar")
        s_hTp = sem("hidden_transposed")
        s_g = sem("gelu_done")
        s_yp = sem("output_product")
        s_ys = sem("output_steps")
        s_yo = sem("output_ready")
        s_out = [sem(f"output_scattered{i}") for i in range(3)]

        block = ctx.enter_context(nc.Block())

        def phases(emit):
            def chunk(eng, c):
                for b in range(B):
                    emit(eng, B * c + b, b, isinstance(c, int) and c == 0 and b == 0,
                         isinstance(c, int) and c == NC - 1 and b == B - 1)

            def program(eng):
                chunk(eng, 0)
                with eng.Fori(1, NC - 1) as c:
                    chunk(eng, c)
                chunk(eng, NC - 1)
            return program

        @block.sync
        def _(eng):
            def load_x(b, c):
                eng.dma_start(xin[:, :, :],
                              xrows[bass.ds(b * T + c * TC, TC), :].rearrange("(i p) d -> p i d", p=P))\
                   .then_inc(s_x, 16)

            def load_res(b, c):
                eng.dma_start(row[:, :, D:2 * D],
                              xrows[bass.ds(b * T + c * TC, TC), :].rearrange("(i p) d -> p i d", p=P))\
                   .then_inc(s_res, 16)

            def store_rows(q, b, c):
                eng.wait_ge(s_xn2, q + 1)
                eng.dma_start(token_rows[bass.ds(b * T + c * TC, TC), :].rearrange("(i p) d -> p i d", p=P),
                              row[:, :, :]).then_inc(s_store, 16)

            eng.dma_start(sm[:, :], small).then_inc(s_small, 16)
            load_x(0, 0)

            def chunk(c):
                for b in range(B):
                    q = B * c + b
                    if not (isinstance(q, int) and q == 0):
                        wait(eng, s_store, 16 * (q - 1))
                        load_res(1 - b, c if b else c - 1)
                    if not (isinstance(c, int) and c == NC - 1):
                        place = 1 if isinstance(q, int) and q == 0 else 3
                        eng.wait_ge(s_full, hop_base(q) + place + 1)
                        load_x(b, c + 1)
                    if not (isinstance(q, int) and q == 0):
                        store_rows(q - 1, 1 - b, c if b else c - 1)

            eng.wait_ge(s_far, 1)
            eng.dma_start(lists.rearrange("(p c) o -> p (c o)", p=P), farf).then_inc(s_init, 16)
            eng.wait_ge(s_full, 2)
            load_x(1, 0)
            chunk(0)
            with eng.Fori(1, NC - 1) as c:
                chunk(c)
            chunk(NC - 1)
            eng.wait_ge(s_store, 16 * (NQ - 1))
            load_res(B - 1, NC - 1)
            store_rows(NQ - 1, B - 1, NC - 1)
            eng.wait_ge(s_y, ITEMS * NQ)
            eng.wait_ge(s_hl, ITEMS * NQ)
            eng.dma_start(w2_sb[:, ring_at:], w2[:, ring_at:]).then_inc(s_w2b, 16)
            eng.wait_ge(s_scat, 16 * TI * NQ)
            eng.dma_start(lists_in.rearrange("p (a c) -> p a c", c=P),
                          lists.rearrange("(a p c) o -> p a (c o)", p=P, c=P)).then_inc(s_lists, 16)

        @block.gpsimd
        def _(eng):
            eng.memset(mhalf[:, :], -0.5).then_inc(s_pconst, 1)
            eng.memset(eps[:, :], EPS).then_inc(s_pconst, 1)
            eng.memset(zero[:, :], 0.0).then_inc(s_pconst, 1)
            eng.memset(ones_bf[:, :], 1.0).then_inc(s_pconst, 1)
            for b in range(B):
                eng.memset(hlast[b][:, :], 0.0).then_inc(s_pconst, 1)
            eng.memset(run[:, :, :], 0.0).then_inc(s_pconst, 1)
            eng.memset(farf, FAR).then_inc(s_far, 1)
            eng.wait_ge(s_pconst, 7)

            own = {"base": 0, "n": 0}

            def rstd(which, count):
                eng.wait_ge(s_var[which], count)
                eng.tensor_tensor(ve[which][:, :], mv[which][:, :, 1], eps[:, :], ALU.add).then_inc(s_eps, 1)
                own["n"] += 1
                eng.wait_ge(s_eps, own["base"] + own["n"])
                eng.tensor_tensor(rs[which][:, :], ve[which][:, :], mhalf[:, :], ALU.pow)\
                   .then_inc(s_rs[which], 1)

            def left(b, which, q1):
                eng.wait_ge(s_part, 3 * q1 + which + 1)
                if which == 0:
                    eng.tensor_tensor(rest[:, :], bc32[:, :], bc3[b][:, :], ALU.subtract).then_inc(s_rest, 1)
                else:
                    eng.tensor_tensor(rest[0:64, :], rest[0:64, :], bc3[b][0:64, :], ALU.subtract)\
                       .then_inc(s_rest, 1)

            def dt_add(b, q1):
                eng.wait_ge(s_pm, q1 + 1)
                eng.tensor_tensor(dts[b][:, :], dts[b][:, :], mag[:, :], ALU.add).then_inc(s_dt, 1)

            def v(q, b, j):
                if j >= ITEMS:
                    q, b, j = q + 1, 1 - b, j - ITEMS
                n, h = divmod(j, KD)
                eng.wait_ge(s_Bsb, N * q + n + 1)
                wait(eng, s_b, ITEMS * q + j - 3)
                eng.tensor_tensor(vb[j % 4], xnT[b][h][:, :], Bsb[n % 4], ALU.mult).then_inc(s_v, 1)

            def enlist(q, b):
                wait_alone(eng, s_slot, q + 1, s_pconst)
                for i in range(TI):
                    eng.indirect_dma_start(
                        out=lists, out_offset=bass.IndirectOffsetOnAxis(ap=slotu[:, i:i + 1], axis=0),
                        in_=tokf[:, b * TI + i:b * TI + i + 1], in_offset=None).then_inc(s_scat, 16)

            def emit(eng, q, b, first, last):
                for j in range(ITEMS):
                    if not last or j + 2 < ITEMS:
                        v(q, b, j + 2)
                    eng.wait_ge(s_h, ITEMS * q + j + 1)
                    eng.tensor_tensor(hlast[b][:, j:j + 1], hb[j % 4][:, TC - 1:TC], zero[:, 0:1], ALU.add)\
                       .then_inc(s_hl, 1)
                    if not last:
                        if j == 4:
                            rstd(0, q + 2)
                        if j == 13:
                            left(1 - b, 0, q + 1)
                        if j == 16:
                            left(1 - b, 1, q + 1)
                        if j == 28:
                            dt_add(1 - b, q + 1)
                    if not first:
                        if j == 9:
                            rstd(1, q)
                        if j == 30:
                            enlist(q - 1, 1 - b)

            rstd(0, 1)
            left(0, 0, 0)
            left(0, 1, 0)
            dt_add(0, 0)
            v(0, 0, 0)
            v(0, 0, 1)
            def chunk(c):
                for b in range(B):
                    q = B * c + b
                    first = isinstance(q, int) and q == 0
                    own["base"], own["n"] = 1 if first else 2 * q, 0
                    emit(eng, q, b, first, isinstance(q, int) and q == NQ - 1)

            chunk(0)
            with eng.Fori(1, NC - 1) as c:
                chunk(c)
            chunk(NC - 1)
            own["base"], own["n"] = 2 * NQ - 1, 0
            rstd(1, NQ)
            enlist(NQ - 1, 1)

            def gather(t, u, r):
                c = eng.value_load(tile_cu[0:1, bass.ds(t, 1)], min_val=0, max_val=E * CAP)
                wait(eng, s_out[u], 16 * r)
                eng.tensor_copy(gcol[u][:, :], ids[:, bass.ds(c, 1)]).then_inc(s_gcol, 1)
                wait_alone(eng, s_gcol, t + 1, s_pconst)
                eng.indirect_dma_start(
                    out=mrow[u], out_offset=None, in_=token_rows,
                    in_offset=bass.IndirectOffsetOnAxis(ap=gcol[u][:, :], axis=0),
                    bounds_check=ROWS - 1, oob_is_err=False).then_inc(s_row[u], 16)

            def b1_copy(t, u):
                wait(eng, s_g, t - 2)
                e = eng.value_load(tile_eu[0:1, bass.ds(t, 1)], min_val=0, max_val=E - 1)
                eng.tensor_copy(b1c[u][:, :], sm[:, bass.ds(e * KH + OFF["b1"][0], KH)]).then_inc(s_b1, 1)

            def put(t, u):
                wait_alone(eng, s_yo, t + 1, s_pconst)
                eng.indirect_dma_start(
                    out=outrows, out_offset=bass.IndirectOffsetOnAxis(ap=gcol[u][:, :], axis=0),
                    in_=yo[u], in_offset=None,
                    bounds_check=ROWS - 1, oob_is_err=False).then_inc(s_out[u], 16)

            eng.wait_ge(s_table, 1)
            eng.wait_ge(s_store, 16 * NQ)
            for u in range(3):
                gather(u, u, 0)
                b1_copy(u, u)

            def step(t, u, r):
                put(t, u)
                if not (isinstance(t, int) and t + 3 >= MT):
                    gather(t + 3, u, r + 1)
                    b1_copy(t + 3, u)

            expert_tiles(eng, step)
            for u in range(3):
                eng.wait_ge(s_out[u], 16 * (MT // 3))

        @block.scalar
        def _(eng):
            eng.dma_start(b2_sb[:, :], b2).then_inc(s_b2, 16)
            for k in range(KD):
                eng.dma_start(w1_sb[:, k, :], w1[:, k, :]).then_inc(s_w, 16)
            eng.dma_start(w2_sb[:, 0:ring_at], w2[:, 0:ring_at]).then_inc(s_w2a, 16)
            eng.wait_ge(s_small, 16)
            eng.activation(negA[:, :], col("logA"), ACT.Exp).then_inc(s_Ae, 1)

            def evac(q, b, name, base, place):
                eng.wait_ge(s_full, base + place + 1)
                if name in ("xn0", "xn1"):
                    h = int(name[-1])
                    wait(eng, s_z, KD * (q - 1))
                    wait(eng, s_v, ITEMS * (q - 1))
                    eng.activation(xnT[b][h][:, :], misc[:, :], ACT.Copy).then_inc(s_free, 1)
                elif name == "bc":
                    eng.activation(bc32[:, :], misc[0:96, :], ACT.Copy).then_inc(s_free, 1)
                    eng.wait_ge(s_free, base + place + 1)
                    wait(eng, s_C, N * (q - 1))
                    eng.activation(bc3[b][:, :], bc32[:, :], ACT.Copy).then_inc(s_part, 1)
                elif name == "dt1":
                    eng.activation(t1[:, :], misc[0:R, :], ACT.Copy).then_inc(s_free, 1)
                elif name in ("dt2_0", "dt2_1"):
                    h = int(name[-1])
                    part = slice(h * TC, (h + 1) * TC)
                    eng.activation(dts[b][:, part], misc[:, :], ACT.Relu, bias=col("bdt2", h, h + 1))
                    eng.activation(mag[:, part], misc[:, :], ACT.Abs, bias=col("bdt2", h, h + 1))\
                       .then_inc(s_free, 1)
                elif name in ("xnr0", "xnr1"):
                    h = int(name[-1])
                    eng.activation(xnrT[h][:, :], misc[:, :], ACT.Copy).then_inc(s_free, 1)

            def parts(q, b, which):
                eng.wait_ge(s_rest, 2 * q + which)
                rows = (64, 32)[which - 1]
                eng.activation(bc3[b][0:rows, :], rest[0:rows, :], ACT.Copy).then_inc(s_part, 1)

            def soft_exp(q, count):
                eng.wait_ge(s_free, count)
                eng.activation(mag[:, :], mag[:, :], ACT.Exp, scale=-1.0).then_inc(s_pms, 1)

            def soft_log(q):
                eng.wait_ge(s_pms, q + 1)
                eng.activation(mag[:, :], mag[:, :], ACT.Ln, bias=1.0).then_inc(s_pm, 1)

            def copy_B(q, b, n):
                if n >= N:
                    q, b, n = q + 1, 1 - b, n - N
                M = N * q + n
                eng.wait_ge(s_Bps, M + 1)
                wait(eng, s_v, KD * (M - 3))
                eng.activation(Bsb[n % 4], Bps[:, :], ACT.Copy).then_inc(s_Bsb, 1)

            def exp_a(q, b, j):
                if j >= ITEMS:
                    q, b, j = q + 1, 1 - b, j - ITEMS
                n, h = divmod(j, KD)
                if j == 0:
                    eng.wait_ge(s_dt, q + 1)
                wait(eng, s_h, ITEMS * q + j - 1)
                eng.activation(A[j % 2][:, :], dts[b][:, h * TC:(h + 1) * TC], ACT.Exp,
                               scale=negA[:, h * N + n:h * N + n + 1]).then_inc(s_a, 1)

            def emit(eng, q, b, first, last):
                at, order = hops(first, last)
                base = hop_base(q)
                for n in range(N):
                    exp_a(q, b, 2 * n + 1)
                    if not last or n + 2 < N:
                        copy_B(q, b, n + 2)
                    if not last or n + 1 < N:
                        exp_a(q, b, 2 * n + 2)
                    name, place = at.get(n, ("", 0))
                    if name in PRE or name in ("xnr0", "xnr1"):
                        if name in PRE:
                            evac(q + 1, 1 - b, name, base, place)
                        else:
                            evac(q - 1, 1 - b, name, base, place)
                    if not last:
                        if n == 7:
                            parts(q + 1, 1 - b, 1)
                        if n == 9:
                            parts(q + 1, 1 - b, 2)
                        if n == 12:
                            soft_exp(q + 1, base + order["dt2_1"] + 1)
                        if n == 13:
                            soft_log(q + 1)
                    if not first and n == 11:
                        softmax_exp(q - 1)

            def softmax_exp(q):
                eng.wait_ge(s_lg, q + 1)
                eng.activation(lg[:, :, :], lg[:, :, :], ACT.Exp).then_inc(s_pe, 1)

            for i, name in enumerate(PRE):
                evac(0, 0, name, 0, i)
                if name == "bc":
                    parts(0, 0, 1)
                    parts(0, 0, 2)
            soft_exp(0, 6)
            soft_log(0)
            eng.wait_ge(s_const, 4)
            copy_B(0, 0, 0)
            copy_B(0, 0, 1)
            exp_a(0, 0, 0)
            phases(emit)(eng)
            evac(NQ - 1, 1, "xnr0", LAST_BASE, 2)
            evac(NQ - 1, 1, "xnr1", LAST_BASE, 3)
            softmax_exp(NQ - 1)

            def copy_hidden(t):
                eng.wait_ge(s_hps, 2 * t + 2)
                eng.activation(hsb[:, H // 2:], hps[:, H // 2:], ACT.Copy).then_inc(s_hB, 1)

            def gelus(t, u):
                eng.wait_ge(s_b1, t + 1)
                wait(eng, s_yp, t)
                for j in range(KH):
                    if j % 4 == 0:
                        eng.wait_ge(s_hTp, 2 * t + j // 4 + 1)
                    g = eng.activation(hT[:, j * P:(j + 1) * P], hTps[:, j * P:(j + 1) * P], ACT.Gelu,
                                       bias=b1c[u][:, j:j + 1])
                g.then_inc(s_g, 1)

            copy_hidden(0)

            def step(t, u, r):
                gelus(t, u)
                if not (isinstance(t, int) and t + 1 >= MT):
                    copy_hidden(t + 1)

            expert_tiles(eng, step)

        @block.tensor
        def _(eng):
            def fill(q, b, name, base, place):
                wait(eng, s_free, base + place)
                if name in ("xn0", "xn1"):
                    h = int(name[-1])
                    eng.wait_ge(s_xn, q + 1)
                    for i in range(TI):
                        mm = eng.transpose(misc[:, i * P:(i + 1) * P], xin[:, i, h * P:(h + 1) * P], ident)
                elif name == "bc":
                    for h in range(KD):
                        mm = eng.matmul(misc[0:96, :], col("wbc", h * 96, h * 96 + 96), xnT[b][h][:, :],
                                        start=(h == 0), stop=(h == KD - 1))
                elif name == "dt1":
                    for h in range(KD):
                        mm = eng.matmul(misc[0:R, :], col("wdt1", h * R, h * R + R), xnT[b][h][:, :],
                                        start=(h == 0), stop=(h == KD - 1))
                elif name in ("dt2_0", "dt2_1"):
                    h = int(name[-1])
                    lo = OFF["wdt2"][0]
                    mm = eng.matmul(misc[:, :], sm[0:R, lo + h * P:lo + (h + 1) * P], t1[:, :],
                                    start=True, stop=True)
                elif name in ("z01", "z23"):
                    eng.wait_ge(s_z, KD * q + KD)
                    for i in range(2):
                        for h in range(KD):
                            a = (i + (2 if name == "z23" else 0)) * P
                            mm = eng.transpose(misc[:, (i * KD + h) * P:(i * KD + h + 1) * P],
                                               z[h][:, a:a + P], ident)
                elif name in ("xnr0", "xnr1"):
                    h = int(name[-1])
                    eng.wait_ge(s_xn2, q + 1)
                    for i in range(TI):
                        mm = eng.transpose(misc[:, i * P:(i + 1) * P], row[:, i, h * P:(h + 1) * P], ident)
                elif name == "route":
                    for i in range(TI):
                        for h in range(KD):
                            mm = eng.matmul(misc[:, i * E:(i + 1) * E], xnrT[h][:, i * P:(i + 1) * P],
                                            col("wr", h * E, (h + 1) * E), start=(h == 0), stop=(h == KD - 1))
                elif name == "rank":
                    eng.wait_ge(s_oh, q + 1)
                    eng.matmul(misc[:, 0:TI * E], tri_bf[:, :], onehot[:, :, :].rearrange("p i e -> p (i e)"),
                               start=True, stop=True)
                    mm = eng.matmul(misc[:, TI * E:2 * TI * E], ones_bf[:, :],
                                    onehot[:, :, :].rearrange("p i e -> p (i e)"), start=True, stop=True)
                mm.then_inc(s_full, 1)

            def spread_B(q, b, n):
                if n >= N:
                    q, b, n = q + 1, 1 - b, n - N
                M = N * q + n
                if n == 0:
                    eng.wait_ge(s_part, 3 * q + 3)
                wait(eng, s_Bsb, M)
                eng.matmul(Bps[:, :], sel[:, n, :], bc3[b][:, :], start=True, stop=True).then_inc(s_Bps, 1)

            def spread_C(q, b, n):
                if n >= N:
                    q, b, n = q + 1, 1 - b, n - N
                M = N * q + n
                wait(eng, s_hc, KD * (M - 1))
                eng.matmul(Cps[n % 2], sel[:, N + n, :], bc3[b][:, :], start=True, stop=True)\
                   .then_inc(s_C, 1)

            def add_y(q, j):
                if j < 0:
                    q, j = q - 1, j + ITEMS
                n, h = divmod(j, KD)
                eng.wait_ge(s_hc, ITEMS * q + j + 1)
                if n == 0:
                    wait(eng, s_z, KD * (q - 1) + h + 1)
                eng.matmul(Y[h], ident, hc[j % 4], start=(n == 0), stop=(n == N - 1)).then_inc(s_y, 1)

            def emit(eng, q, b, first, last):
                at, order = hops(first, last)
                base = hop_base(q)
                for n in range(N):
                    if not last or n + 1 < N:
                        spread_C(q, b, n + 1)
                    if not last or n + 2 < N:
                        spread_B(q, b, n + 2)
                    if n in at:
                        name, place = at[n]
                        if name in PRE:
                            fill(q + 1, 1 - b, name, base, place)
                        else:
                            fill(q - 1, 1 - b, name, base, place)
                    if n > 0 or not first:
                        add_y(q, 2 * n - 2)
                        add_y(q, 2 * n - 1)

            eng.wait_ge(s_small, 16)
            for i, name in enumerate(PRE):
                fill(0, 0, name, 0, i)
            eng.wait_ge(s_const, 4)
            spread_B(0, 0, 0)
            spread_C(0, 0, 0)
            spread_B(0, 0, 1)
            phases(emit)(eng)
            add_y(NQ, -2)
            add_y(NQ, -1)
            for i, name in enumerate(POST):
                fill(NQ - 1, 1, name, LAST_BASE, i)
            eng.wait_ge(s_lists, 16)
            eng.wait_ge(s_slot, NQ)
            for i in range(E * CAP // P):
                mm = eng.transpose(misc[:, i * P:(i + 1) * P], lists_in[:, i * P:(i + 1) * P], ident)
            mm.then_inc(s_lt, 1)

            def turn_x(t, u, r):
                eng.wait_ge(s_row[u], 16 * (r + 1))
                wait(eng, s_xT, t)
                for h in range(KD):
                    mm = eng.transpose(xTps[:, h * P:(h + 1) * P], mrow[u][:, h * P:(h + 1) * P], ident)
                mm.then_inc(s_xTp, 1)

            def hidden(t):
                e = eng.value_load(tile_eu[0:1, bass.ds(t, 1)], min_val=0, max_val=E - 1)
                eng.wait_ge(s_xT, t + 1)
                for s in range(2):
                    wait(eng, (s_hA, s_hB)[s], t)
                    for h in range(KD):
                        mm = eng.matmul(hps[:, s * 512:(s + 1) * 512], xT[:, h * P:(h + 1) * P],
                                        w1_sb[:, h, bass.ds(e * H + s * 512, 512)],
                                        start=(h == 0), stop=(h == KD - 1))
                    mm.then_inc(s_hps, 1)

            def turn_h(t):
                wait(eng, s_g, t)
                for j in range(KH):
                    if j == 0:
                        eng.wait_ge(s_hA, t + 1)
                    if j == 4:
                        eng.wait_ge(s_hB, t + 1)
                    mm = eng.transpose(hTps[:, j * P:(j + 1) * P], hsb[:, j * P:(j + 1) * P], ident)
                    if j % 4 == 3:
                        mm.then_inc(s_hTp, 1)

            def outputs(t):
                e = eng.value_load(tile_eu[0:1, bass.ds(t, 1)], min_val=0, max_val=E - 1)
                eng.wait_ge(s_g, t + 1)
                wait(eng, s_ys, t)
                for j in range(KH):
                    mm = eng.matmul(yps[:, 0:D], hT[:, j * P:(j + 1) * P],
                                    w2_sb[:, bass.ds(e * KH * D + j * D, D)],
                                    start=(j == 0), stop=(j == KH - 1))
                mm.then_inc(s_yp, 1)

            eng.wait_ge(s_table, 1)
            eng.wait_ge(s_w, 16 * KD)
            turn_x(0, 0, 0)
            hidden(0)
            turn_x(1, 1, 0)
            eng.wait_ge(s_w2a, 16)
            eng.wait_ge(s_w2b, 16)

            def step(t, u, r):
                turn_h(t)
                if not (isinstance(t, int) and t + 1 >= MT):
                    hidden(t + 1)
                if not (isinstance(t, int) and t + 2 >= MT):
                    turn_x(t + 2, (u + 2) % 3, r + (u + 2) // 3)
                outputs(t)

            expert_tiles(eng, step)

        @block.vector
        def _(eng):
            own = {"ln": 0, "rt": 0, "tab": 0}
            sems = {"ln": s_ln, "rt": s_rt, "tab": s_tab}
            bases = {"ln": 0, "rt": 0, "tab": 0}

            def done(ins, kind):
                ins.then_inc(sems[kind], 1)
                own[kind] += 1
                eng.wait_ge(sems[kind], bases[kind] + own[kind])

            eng.wait_ge(s_small, 16)
            eng.wait_ge(s_Ae, 1)
            done(eng.tensor_scalar(negA[:, :], negA[:, :], -1.0, None, ALU.mult), "tab")
            done(eng.tensor_scalar(invA[:, :], negA[:, :], 1e-8, None, ALU.add), "tab")
            eng.reciprocal(invA[:, :], invA[:, :]).then_inc(s_const, 1)
            eng.tensor_copy(sel[:, :, :], sm[0:96, OFF["spread"][0]:OFF["spread"][1]].unsqueeze(2)
                            .to_broadcast([96, 32, P])).then_inc(s_const, 1)
            eng.tensor_copy(tri_bf[:, :], col("tri")).then_inc(s_const, 1)
            eng.tensor_copy(tokf[:, :], col("tok0")).then_inc(s_const, 1)

            def stats(which, i, src):
                eng.bn_stats(st[which][:, i * 6:(i + 1) * 6], src).then_inc(s_ln, 1)
                own["ln"] += 1

            def aggregate(which):
                wait_alone(eng, s_ln, bases["ln"] + own["ln"], s_small)
                for i in range(TI):
                    ins = eng.bn_aggr(mv[which][:, i, :], st[which][:, i * 6:(i + 1) * 6])
                ins.then_inc(s_var[which], 1)

            def normalise(which, count, src, dst, signal):
                eng.wait_ge(s_rs[which], count)
                for i in range(TI):
                    ins = eng.tensor_scalar(dst(i), src(i), mv[which][:, i, 0:1], rs[which][:, i:i + 1],
                                            ALU.subtract, ALU.mult)
                ins.then_inc(signal, 1)

            def ln1_stats(q):
                eng.wait_ge(s_x, 16 * (q + 1))
                for i in range(TI):
                    stats(0, i, xin[:, i, :])
                aggregate(0)

            def ln1_norm(q):
                normalise(0, q + 1, lambda i: xin[:, i, :], lambda i: xin[:, i, :], s_xn)

            def make_b(q, b, j):
                if j >= ITEMS:
                    q, b, j = q + 1, 1 - b, j - ITEMS
                k = ITEMS * q + j
                eng.wait_ge(s_a, k + 1)
                eng.wait_ge(s_v, k + 1)
                eng.scalar_tensor_tensor(bb[j % 2][:, :], A[j % 2][:, :], 1.0, vb[j % 4],
                                         ALU.subtract, ALU.mult).then_inc(s_b, 1)

            def scan(q, b, j):
                k = ITEMS * q + j
                eng.wait_ge(s_b, k + 1)
                wait(eng, s_hl, k - 3)
                eng.tensor_tensor_scan(hb[j % 4], A[j % 2][:, :], bb[j % 2][:, :], hlast[b][:, j:j + 1],
                                       ALU.mult, ALU.add).then_inc(s_h, 1)

            def make_hc(q, b, j):
                if j < 0:
                    q, b, j = q - 1, 1 - b, j + ITEMS
                n, h = divmod(j, KD)
                k = ITEMS * q + j
                eng.wait_ge(s_h, k + 1)
                eng.wait_ge(s_C, N * q + n + 1)
                wait(eng, s_y, k - 3)
                eng.scalar_tensor_tensor(hc[j % 4], hb[j % 4], invA[:, h * N + n:h * N + n + 1],
                                         Cps[n % 2], ALU.mult, ALU.mult).then_inc(s_hc, 1)

            def make_z(q, b):
                for h in range(KD):
                    eng.wait_ge(s_y, ITEMS * q + ITEMS - 1 + h)
                    eng.scalar_tensor_tensor(z[h][:, :], xnT[b][h][:, :], col("dskip", h, h + 1), Y[h],
                                             ALU.mult, ALU.add).then_inc(s_z, 1)

            def add_residual(q, which, base, place):
                eng.wait_ge(s_full, base + place + 1)
                eng.wait_ge(s_res, 16 * (q + 1))
                dst = row[:, 2 * which:2 * which + 2, D:2 * D]
                eng.tensor_tensor(dst, misc[:, :].rearrange("p (i d) -> p i d", i=2), dst, ALU.add)\
                   .then_inc(s_free, 1)
                eng.wait_ge(s_free, base + place + 1)
                for i in range(2 * which, 2 * which + 2):
                    stats(1, i, row[:, i, D:2 * D])

            def ln2_norm(q):
                normalise(1, q + 1, lambda i: row[:, i, D:2 * D], lambda i: row[:, i, 0:D], s_xn2)

            def over_e(ap):
                return ap.unsqueeze(2).to_broadcast([P, TI, E])

            def logits(q, base, place):
                eng.wait_ge(s_full, base + place + 1)
                eng.tensor_tensor(lg[:, :, :], misc[:, 0:TI * E].rearrange("p (i e) -> p i e", e=E),
                                  col("br").unsqueeze(1).to_broadcast([P, TI, E]), ALU.add)\
                   .then_inc(s_free, 1)
                eng.wait_ge(s_free, base + place + 1)
                done(eng.tensor_reduce(red[:, :], lg[:, :, :], AX.X, ALU.max), "rt")
                eng.tensor_tensor(lg[:, :, :], lg[:, :, :], over_e(red[:, :]), ALU.subtract).then_inc(s_lg, 1)

            def choose(q):
                eng.wait_ge(s_pe, q + 1)
                done(eng.tensor_reduce(red[:, :], lg[:, :, :], AX.X, ALU.add), "rt")
                done(eng.reciprocal(red[:, :], red[:, :]), "rt")
                done(eng.tensor_tensor(lg[:, :, :], lg[:, :, :], over_e(red[:, :]), ALU.mult), "rt")
                done(eng.tensor_reduce(red[:, :], lg[:, :, :], AX.X, ALU.max), "rt")
                done(eng.tensor_tensor(lg[:, :, :], lg[:, :, :], over_e(red[:, :]), ALU.is_equal), "rt")
                less8 = col("e_less8").unsqueeze(1).to_broadcast([P, TI, E])
                done(eng.tensor_tensor(lg[:, :, :], lg[:, :, :], less8, ALU.mult), "rt")
                done(eng.tensor_reduce(pick[:, :], lg[:, :, :], AX.X, ALU.min), "rt")
                eng.tensor_tensor(onehot[:, :, :], over_e(pick[:, :]), less8, ALU.is_equal).then_inc(s_oh, 1)

            def place_tokens(q, b, base, place):
                eng.wait_ge(s_full, base + place + 1)
                done(eng.tensor_copy(run[:, 0, :], run[:, TI, :]), "rt")
                for i in range(TI):
                    done(eng.tensor_tensor(run[:, i + 1, :], run[:, i, :],
                                           misc[:, (TI + i) * E:(TI + i + 1) * E], ALU.add), "rt")
                eng.tensor_tensor(slot[:, :, :], misc[:, 0:TI * E].rearrange("p (i e) -> p i e", e=E),
                                  run[:, 0:TI, :], ALU.add).then_inc(s_free, 1)
                eng.wait_ge(s_free, base + place + 1)
                ebase = col("e_base").unsqueeze(1).to_broadcast([P, TI, E])
                done(eng.tensor_tensor(slot[:, :, :], slot[:, :, :], ebase, ALU.add), "rt")
                done(eng.tensor_tensor(slot[:, :, :], slot[:, :, :], onehot[:, :, :], ALU.mult), "rt")
                done(eng.tensor_reduce(slotf[:, :], slot[:, :, :], AX.X, ALU.add), "rt")
                wait(eng, s_scat, 16 * TI * q)
                eng.tensor_scalar(tokf[:, b * TI:(b + 1) * TI], tokf[:, b * TI:(b + 1) * TI], float(TC),
                                  None, ALU.add)
                eng.tensor_copy(slotu[:, :], slotf[:, :]).then_inc(s_slot, 1)

            def emit(eng, q, b, first, last):
                at, order = hops(first, last)
                base = hop_base(q)
                bases["ln"], own["ln"] = TI if first else 2 * TI * q, 0
                bases["rt"], own["rt"] = RT_STEPS * (q - 1), 0
                for j in range(ITEMS):
                    scan(q, b, j)
                    if not last or j + 1 < ITEMS:
                        make_b(q, b, j + 1)
                    if not (first and j == 0):
                        make_hc(q, b, j - 1)
                    if not first:
                        if j == 2:
                            make_z(q - 1, 1 - b)
                        if j == 5:
                            add_residual(q - 1, 0, base, order["z01"])
                        if j == 7:
                            add_residual(q - 1, 1, base, order["z23"])
                            aggregate(1)
                        if j == 11:
                            ln2_norm(q - 1)
                        if j == 20:
                            logits(q - 1, base, order["route"])
                        if j == 24:
                            choose(q - 1)
                        if j == 28:
                            place_tokens(q - 1, 1 - b, base, order["rank"])
                    if not last:
                        if j == 3:
                            ln1_stats(q + 1)
                        if j == 6:
                            ln1_norm(q + 1)

            ln1_stats(0)
            ln1_norm(0)
            assert own["ln"] == TI
            eng.wait_ge(s_pconst, 7)
            eng.wait_ge(s_init, 16)
            make_b(0, 0, 0)
            phases(emit)(eng)
            make_hc(NQ, 0, -1)
            bases["ln"], own["ln"] = 2 * TI * NQ - TI, 0
            bases["rt"], own["rt"] = RT_STEPS * (NQ - 1), 0
            q = NQ - 1
            make_z(q, 1)
            add_residual(q, 0, LAST_BASE, 0)
            add_residual(q, 1, LAST_BASE, 1)
            aggregate(1)
            ln2_norm(q)
            logits(q, LAST_BASE, 4)
            choose(q)
            place_tokens(q, 1, LAST_BASE, 5)

            cnt = run[:, TI, :]
            g1 = big[:, 0:E * 32].rearrange("p (e j) -> p e j", j=32)
            done(eng.tensor_tensor(g1, cnt.unsqueeze(2).to_broadcast([P, E, 32]),
                                   col("j128").unsqueeze(1).to_broadcast([P, E, 32]), ALU.is_gt), "tab")
            done(eng.tensor_reduce(ntile[:, :], g1, AX.X, ALU.add), "tab")
            done(eng.memset(cum[:, 0:1], 0.0), "tab")
            for e in range(E):
                done(eng.tensor_tensor(cum[:, e + 1:e + 2], cum[:, e:e + 1], ntile[:, e:e + 1], ALU.add),
                     "tab")
            g2 = big[:, 0:MT * E].rearrange("p (k e) -> p k e", e=E)
            g3 = big2[:, 0:MT * E].rearrange("p (k e) -> p k e", e=E)
            no = col("tile_no").unsqueeze(2).to_broadcast([P, MT, E])

            def over_k(ap):
                return ap.unsqueeze(1).to_broadcast([P, MT, E])

            done(eng.tensor_tensor(g2, over_k(cum[:, 1:E + 1]), no, ALU.is_le), "tab")
            done(eng.tensor_reduce(tile_e[:, :], g2, AX.X, ALU.add), "tab")
            done(eng.tensor_tensor(g3, g2, over_k(ntile[:, :]), ALU.mult), "tab")
            done(eng.tensor_reduce(tile_c[:, :], g3, AX.X, ALU.add), "tab")
            done(eng.tensor_tensor(tile_c[:, :], col("tile_no"), tile_c[:, :], ALU.subtract), "tab")
            done(eng.scalar_tensor_tensor(tile_c[:, :], tile_e[:, :], float(CAP), tile_c[:, :],
                                          ALU.mult, ALU.add), "tab")
            done(eng.tensor_scalar(tile_cu[:, :], tile_c[:, :], float(E * CAP), None, ALU.min), "tab")
            done(eng.tensor_scalar(tile_eu[:, :], tile_e[:, :], float(E - 1), None, ALU.min), "tab")
            done(eng.memset(red[:, 0:1], FAR), "tab")
            done(eng.tensor_copy(ids[:, E * CAP:E * CAP + 1], red[:, 0:1]), "tab")
            eng.wait_ge(s_lt, 1)
            eng.tensor_copy(ids[:, 0:E * CAP], misc[:, 0:E * CAP]).then_inc(s_table, 1)

            def copy_xT(t):
                eng.wait_ge(s_xTp, t + 1)
                wait(eng, s_hps, 2 * t)
                eng.tensor_copy(xT, xTps[:, 0:D]).then_inc(s_xT, 1)

            def copy_hidden(t):
                eng.wait_ge(s_hps, 2 * t + 1)
                wait(eng, s_hTp, 2 * t)
                eng.tensor_copy(hsb[:, 0:H // 2], hps[:, 0:H // 2]).then_inc(s_hA, 1)

            def finish(t, u, r):
                e = eng.value_load(tile_eu[0:1, bass.ds(t, 1)], min_val=0, max_val=E - 1)
                eng.wait_ge(s_yp, t + 1)
                wait(eng, s_out[u], 16 * r)
                eng.tensor_tensor(yo[u], yps[:, 0:D], b2_sb[:, bass.ds(e * D, D)], ALU.add)\
                   .then_inc(s_ys, 1)
                eng.wait_ge(s_ys, t + 1)
                eng.tensor_tensor(yo[u], yo[u], mrow[u][:, D:2 * D], ALU.add).then_inc(s_yo, 1)

            eng.wait_ge(s_table, 1)
            eng.wait_ge(s_b2, 16)
            copy_xT(0)
            copy_hidden(0)
            copy_xT(1)

            def step(t, u, r):
                if not (isinstance(t, int) and t + 1 >= MT):
                    copy_hidden(t + 1)
                if not (isinstance(t, int) and t + 2 >= MT):
                    copy_xT(t + 2)
                finish(t, u, r)

            expert_tiles(eng, step)


def kernel(**inputs):
    import concourse.bacc as bacc
    from concourse.bass_utils import run_bass_kernel_spmd

    a = {k.removeprefix("L0_"): np.asarray(v) for k, v in inputs.items()}

    def halves(w):
        return w.reshape(KD, P, -1).transpose(1, 0, 2).reshape(P, -1)

    def pad(w):
        return np.concatenate([w, np.zeros((P - w.shape[0], w.shape[1]), np.float32)])

    f = np.float32
    one = np.arange(P)
    bc = np.concatenate([a["attn_W_B"], a["attn_W_C"]]).T
    parts = dict(
        ident=np.eye(P, dtype=f), logA=halves(a["attn_log_A"]), bdt2=halves(a["attn_b_dt2"][:, None]),
        dskip=halves(a["attn_D_skip"][:, None]), wr=halves(a["ffn_Wr"]),
        wbc=halves(np.concatenate([bc, bc, bc], axis=1)), wdt1=halves(a["attn_W_dt1"].T),
        wdt2=pad(a["attn_W_dt2"].T),
        b1=a["ffn_b1"].reshape(E, KH, P).transpose(2, 0, 1).reshape(P, -1),
        tri=(one[:, None] < one[None, :]).astype(f),
        spread=pad((np.arange(96)[:, None] % 32 == np.arange(32)[None, :]).astype(f)),
        e_less8=np.tile(np.arange(E, dtype=f) - E, (P, 1)),
        e_base=np.tile(np.arange(E, dtype=f) * ROWS, (P, 1)),
        tok0=(np.arange(B)[None, :, None] * T + np.arange(TI)[None, None, :] * P - TC
              + one[:, None, None]).reshape(P, -1).astype(f),
        j128=np.tile(np.arange(32, dtype=f) * P, (P, 1)),
        tile_no=np.tile(np.arange(MT, dtype=f), (P, 1)),
        br=np.tile(a["ffn_br"], (P, 1)))
    assert list(parts) == list(SMALL)
    arrays = {
        "x_in": np.ascontiguousarray(a["attn_x"]),
        "small_in": np.ascontiguousarray(np.concatenate(list(parts.values()), axis=1)),
        "w1_in": np.ascontiguousarray(
            a["ffn_W1"].reshape(E, KD, P, H).transpose(2, 1, 0, 3).reshape(P, KD, E * H)),
        "w2_in": np.ascontiguousarray(
            a["ffn_W2"].reshape(E, KH, P, D).transpose(2, 0, 1, 3).reshape(P, E * KH * D)),
        "b2_in": np.ascontiguousarray(np.tile(a["ffn_b2"].reshape(1, -1), (P, 1))),
    }
    nc = bacc.Bacc("TRN2", target_bir_lowering=False, num_devices=1)
    args = [nc.dram_tensor(n, v.shape, mybir.dt.from_np(v.dtype), kind="ExternalInput").ap()
            for n, v in arrays.items()]
    out = nc.dram_tensor("y_out", (B, T, D), F32, kind="ExternalOutput").ap()
    build(nc, *args, out)
    r = run_bass_kernel_spmd(nc, [arrays], core_ids=[0])
    return r.results[0]["y_out"]
```

```python
from contextlib import ExitStack

import numpy as np

import concourse.bass as bass
from concourse import mybir

F32 = mybir.dt.float32
BF16 = mybir.dt.bfloat16
U32 = mybir.dt.uint32
ALU = mybir.AluOpType
ACT = mybir.ActivationFunctionType
AX = mybir.AxisListType

P = 128
B, T, D = 2, 2048, 256
N = 16
R = 64
E, H = 8, 1024
ROWS = B * T
TC = 512
NC = T // TC
NQ = B * NC
TI = TC // P
KD = D // P
KH = H // P
ITEMS = N * KD
POOLED = (2, 3, 4, 6, 7, 10, 11, 12)
MT = ROWS // P + E - 1
CAP = ROWS // P
FAR = 1.0e6
EPS = 1e-5

SMALL = dict(ident=P, logA=KD * N, bdt2=KD, dskip=KD, wr=KD * E, wbc=KD * 96, wdt1=KD * R, wdt2=D,
             b1=E * KH, tri=P, spread=32, e_less8=E, e_base=E, tok0=B * TI, j128=32, tile_no=MT, br=E)
OFF = {}
_at = 0
for _name, _w in SMALL.items():
    OFF[_name] = (_at, _at + _w)
    _at += _w
SW = _at

POST = {"z01": 2, "z23": 3, "xnr0": 8, "xnr1": 9, "route": 10, "rank": 14}
PRE = {"xn0": 4, "xn1": 5, "bc": 6, "dt1": 7, "dt2_0": 11, "dt2_1": 12}
LAST_BASE = 12 * NQ - 6
RT_STEPS = 15


def hops(first, last):
    names = ({} if first else POST) | ({} if last else PRE)
    order = sorted(names, key=names.get)
    return {names[x]: (x, i) for i, x in enumerate(order)}, {x: i for i, x in enumerate(order)}


def hop_base(q):
    return 6 if isinstance(q, int) and q == 0 else 12 * q


def wait(eng, sem, value):
    if not (isinstance(value, int) and value <= 0):
        eng.wait_ge(sem, value)


def pooled(n, h):
    return h == KD - 1 and n in POOLED


def made_before(j):
    return j - sum(KD * n + KD - 1 < j for n in POOLED)


assert len(POOLED) % 2 == 0
VECTOR_ITEMS = made_before(ITEMS)


def wait_alone(eng, sem, value, met):
    value = value if isinstance(value, int) else eng.to_reg(value)
    eng.wait_ge(met, 1)
    eng.wait_ge(sem, value)


def expert_tiles(eng, step):
    for u in range(4):
        step(u, u, 0)
    with eng.Fori(1, MT // 4) as r:
        for u in range(4):
            step(4 * r + u, u, r)
    for u in range(MT % 4):
        step(MT - MT % 4 + u, u, MT // 4)


def build(nc, x, small, w1, w2, b2, out):
    with ExitStack() as ctx:
        def sb(name, shape, dt=F32):
            return ctx.enter_context(nc.sbuf_tensor(name, shape, dt))

        def ps(name, shape):
            return ctx.enter_context(nc.psum_tensor(name, shape, F32))

        def sem(name):
            return ctx.enter_context(nc.semaphore(name))

        xrows = x.rearrange("b t d -> (b t) d")
        outrows = out.rearrange("b t d -> (b t) d")
        token_rows = nc.dram_tensor("token_rows", [ROWS, 2 * D], F32, kind="Internal").ap()
        lists = nc.dram_tensor("lists", [E * ROWS, 1], F32, kind="Internal").ap()

        sm = sb("sm", [P, SW])

        def col(name, a=0, b=None):
            lo, hi = OFF[name]
            return sm[:, lo + a:(hi if b is None else lo + b)]

        ident = col("ident")
        w1_sb = sb("w1_sb", [P, KD, E * H])
        w2_sb = sb("w2_sb", [P, E * KH * D])
        b2_sb = sb("b2_sb", [P, E * D])
        negA = sb("negA", [P, KD * N])
        invA = sb("invA", [P, KD * N])
        dskip = sb("dskip", [P, KD, P])
        tri_bf = sb("tri_bf", [P, P], BF16)
        ones_bf = sb("ones_bf", [P, P], BF16)
        sel = sb("sel", [96, 32, P], BF16)

        def x_ahead(q):
            half, at = divmod((q - 1) * TI * D, E * H)
            return w1_sb[:, half, at:at + TI * D].rearrange("p (i d) -> p i d", d=D)

        ring_at = (E // 2) * KH * D

        def ring(i, j):
            a = ring_at + (4 * i + j) * TC
            return w2_sb[:, a:a + TC]

        def pair(i, n):
            a = ring_at + (4 * i + KD * n % 4) * TC
            return w2_sb[:, a:a + KD * TC]

        Bsb = [ring(0, j) for j in range(4)]
        vb = [ring(1, j) for j in range(4)]
        hb = [ring(2, j) for j in range(4)]
        hc = [ring(3, j) for j in range(4)]
        Csb = [sb(f"Csb{i}", [P, TC]) for i in range(2)]
        bb = [sb(f"b{i}", [P, TC]) for i in range(2)]
        xin = sb("xin", [P, TI, D])
        xnTs = [sb(f"xnT{b}", [P, KD * TC]) for b in range(B)]
        xnT = [[xnTs[b][:, h * TC:(h + 1) * TC] for h in range(KD)] for b in range(B)]
        dts = [sb(f"dt{b}", [P, KD * TC]) for b in range(B)]
        mag = sb("mag", [P, KD * TC])
        bc32 = mag[0:96, 0:TC]
        rest = mag[0:96, TC:2 * TC]
        bc3 = [sb(f"bc3_{b}", [96, TC], BF16) for b in range(B)]
        t1 = sb("t1", [R, TC])
        hlast = [sb(f"hlast{b}", [P, ITEMS]) for b in range(B)]
        z = [sb(f"z{h}", [P, TC]) for h in range(KD)]
        row = sb("row", [P, TI, 2 * D])
        xnrTs = sb("xnrT", [P, KD * TC])
        xnrT = [xnrTs[:, h * TC:(h + 1) * TC] for h in range(KD)]
        st = [sb(f"st{i}", [P, TI * 6]) for i in range(2)]
        mv = [sb(f"mv{i}", [P, TI, 2]) for i in range(2)]
        ve = [sb(f"ve{i}", [P, TI]) for i in range(2)]
        rs = [sb(f"rs{i}", [P, TI]) for i in range(2)]
        nm = [sb(f"nm{i}", [P, TI]) for i in range(2)]
        AH = (NQ - 1) * TI
        stx = sb("stx", [P, AH * 6])
        mvx = sb("mvx", [P, AH, 2])
        vex = sb("vex", [P, AH])
        nmx = sb("nmx", [P, AH])
        rnx = sb("rnx", [P, NQ - 1, 2 * TI])
        rn = [sb(f"rn{b}", [P, 2 * TI]) for b in range(B)]
        mhalf = sb("mhalf", [P, TI])
        eps = sb("eps", [P, AH])
        zero = sb("zero", [P, 1])
        lg = sb("lg", [P, TI, E])
        red = sb("red", [P, TI])
        pick = sb("pick", [P, TI])
        onehot = sb("onehot", [P, TI, E], BF16)
        run = sb("run", [P, TI + 1, E])
        slot = sb("slot", [P, TI, E])
        slotf = sb("slotf", [P, TI])
        slotu = sb("slotu", [P, TI], U32)
        tokf = sb("tokf", [P, B * TI])

        hT = [dts[0][:, :], dts[1][:, :]]
        xT = [z[0][:, 0:D], z[0][:, D:2 * D]]
        w1c = [[xnTs[0], xnTs[1]],
               [xin[:, :, :].rearrange("p i d -> p (i d)"), xnrTs]]
        yo = [mag[:, i * D:(i + 1) * D] for i in range(4)]
        mrow = [row[:, i, :] for i in range(4)]
        b1c = [sb(f"b1c{i}", [P, KH]) for i in range(4)]
        gcol = [sb(f"gcol{i}", [P, 1], U32) for i in range(4)]
        cum = sb("cum", [P, E + 1])
        ntile = sb("ntile", [P, E])
        ntok = sb("ntok", [P, E])
        big = bb[0]
        big2 = bb[1]
        tile_e = sb("tile_e", [P, MT])
        tile_c = sb("tile_c", [P, MT])
        tile_eu = sb("tile_eu", [P, MT], U32)
        tile_cu = sb("tile_cu", [P, MT], U32)
        lists_in = z[1][:, 0:E * CAP]
        farf = z[1][:, E * CAP:2 * E * CAP]
        ids = sb("ids", [P, E * CAP + 1], U32)

        bank = [ps(f"bank{i}", [P, 512]) for i in range(3)]
        A = [bank[0], bank[1]]
        Bps = bank[2]
        misc = ps("misc", [P, 512])
        CC = ps("CC", [P, 1024])
        YY = ps("YY", [P, 1024])
        Cps = [CC[:, 0:512], CC[:, 512:1024]]
        Y = [YY[:, 0:512], YY[:, 512:1024]]
        start_bank = dict(xn0=misc, xn1=Y[0], bc=Y[1], dt1=misc, dt2_0=Y[0], dt2_1=Cps[1])
        last_bank = dict.fromkeys(POST, misc) | dict(z23=bank[0], xnr1=bank[0])
        hps = [CC[:, :], YY[:, :]]
        xTps = [bank[0], bank[2]]
        yps = [bank[1], misc]

        s_small = sem("small_loaded")
        s_w = sem("w1_loaded")
        s_w2a = sem("w2_lower_loaded")
        s_w2b = sem("w2_upper_loaded")
        s_b2 = sem("b2_loaded")
        s_x = sem("x_loaded")
        s_ahead = [sem(f"x_ahead_loaded{q}") for q in range(1, NQ)]
        s_varx = sem("variances_ahead")
        s_rsx = sem("rstd_ahead")
        s_rn = sem("rstd_copied")
        s_res = sem("residual_loaded")
        s_const = sem("constants_built")
        s_pconst = sem("gpsimd_constants_built")
        s_Ae = sem("A_exponent")
        s_xn = sem("layernorm1_done")
        s_var = [sem("variance1"), sem("variance2")]
        s_rs = [sem("rstd1"), sem("rstd2")]
        s_ln = sem("layernorm_steps")
        s_full = sem("shared_bank_filled")
        s_free = sem("shared_bank_read")
        s_part = sem("bc_parts_rounded")
        s_rest = sem("bc_parts_left")
        s_pm = sem("softplus_log")
        s_pms = sem("softplus_exp")
        s_dt = sem("dt_ready")
        s_Bps = sem("B_spread")
        s_Bsb = sem("B_copied")
        s_C = sem("C_spread")
        s_a = sem("a_ready")
        s_v = sem("v_ready")
        s_b = sem("b_ready")
        s_h = sem("h_ready")
        s_hl = sem("h_last_kept")
        s_hc = sem("hC_ready")
        s_Cs = sem("C_copied")
        s_hcp = sem("hC_ready_gpsimd")
        s_y = sem("y_added")
        s_z = sem("z_ready")
        s_eps = sem("eps_added")
        s_xn2 = sem("layernorm2_done")
        s_lg = sem("logits_centred")
        s_pe = sem("exponentials")
        s_rt = sem("routing_steps")
        s_oh = sem("onehot_ready")
        s_slot = sem("slots_ready")
        s_far = sem("far_filled")
        s_init = sem("lists_started")
        s_store = sem("token_rows_stored")
        s_scat = sem("tokens_listed")
        s_lists = sem("lists_loaded")
        s_lt = sem("lists_transposed")
        s_tab = sem("table_steps")
        s_table = sem("table_ready")
        s_gcol = sem("gather_index_copied")
        s_row = [sem(f"rows_gathered{i}") for i in range(4)]
        s_b1 = sem("b1_copied")
        s_xTp = sem("xT_transposed")
        s_xT = sem("xT_copied")
        s_w1c = sem("w1_copied")
        s_hps = sem("hidden_product")
        s_g = sem("gelu_done")
        s_yp = sem("output_product")
        s_ys = sem("output_steps")
        s_yo = sem("output_ready")
        s_out = [sem(f"output_scattered{i}") for i in range(4)]

        block = ctx.enter_context(nc.Block())

        def phases(emit):
            def chunk(eng, c):
                for b in range(B):
                    emit(eng, B * c + b, b, isinstance(c, int) and c == 0 and b == 0,
                         isinstance(c, int) and c == NC - 1 and b == B - 1)

            def program(eng):
                chunk(eng, 0)
                with eng.Fori(1, NC - 1) as c:
                    chunk(eng, c)
                chunk(eng, NC - 1)
            return program

        @block.sync
        def _(eng):
            def load_x(b, c):
                eng.dma_start(xin[:, :, :],
                              xrows[bass.ds(b * T + c * TC, TC), :].rearrange("(i p) d -> p i d", p=P))\
                   .then_inc(s_x, 16)

            def load_res(b, c):
                eng.dma_start(row[:, :, D:2 * D],
                              xrows[bass.ds(b * T + c * TC, TC), :].rearrange("(i p) d -> p i d", p=P))\
                   .then_inc(s_res, 16)

            def store_rows(q, b, c):
                eng.wait_ge(s_xn2, q + 1)
                eng.dma_start(token_rows[bass.ds(b * T + c * TC, TC), :].rearrange("(i p) d -> p i d", p=P),
                              row[:, :, :]).then_inc(s_store, 16)

            load_x(0, 0)
            eng.dma_start(sm[:, :], small).then_inc(s_small, 16)

            def chunk(c):
                for b in range(B):
                    q = B * c + b
                    if not (isinstance(q, int) and q == 0):
                        wait(eng, s_store, 16 * (q - 1))
                        load_res(1 - b, c if b else c - 1)
                    if not (isinstance(c, int) and c == NC - 1):
                        place = 1 if isinstance(q, int) and q == 0 else 3
                        eng.wait_ge(s_full, hop_base(q) + place + 1)
                        load_x(b, c + 1)
                    if not (isinstance(q, int) and q == 0):
                        store_rows(q - 1, 1 - b, c if b else c - 1)

            eng.wait_ge(s_far, 1)
            eng.dma_start(lists.rearrange("(p c) o -> p (c o)", p=P), farf).then_inc(s_init, 16)
            for q in range(1, NQ):
                eng.dma_start(x_ahead(q), xrows[q % B * T + q // B * TC:q % B * T + (q // B + 1) * TC, :]
                              .rearrange("(i p) d -> p i d", p=P)).then_inc(s_ahead[q - 1], 16)
            eng.wait_ge(s_full, 2)
            load_x(1, 0)
            chunk(0)
            with eng.Fori(1, NC - 1) as c:
                chunk(c)
            chunk(NC - 1)
            eng.wait_ge(s_store, 16 * (NQ - 1))
            load_res(B - 1, NC - 1)
            store_rows(NQ - 1, B - 1, NC - 1)
            eng.wait_ge(s_y, ITEMS * NQ)
            eng.wait_ge(s_hl, N * NQ)
            eng.dma_start(w2_sb[:, ring_at:], w2[:, ring_at:]).then_inc(s_w2b, 16)
            eng.wait_ge(s_scat, 16 * TI * NQ)
            eng.dma_start(lists_in.rearrange("p (a c) -> p a c", c=P),
                          lists.rearrange("(a p c) o -> p a (c o)", p=P, c=P)).then_inc(s_lists, 16)

        @block.gpsimd
        def _(eng):
            eng.memset(mhalf[:, :], -0.5).then_inc(s_pconst, 1)
            eng.memset(eps[:, :], EPS).then_inc(s_pconst, 1)
            eng.memset(zero[:, :], 0.0).then_inc(s_pconst, 1)
            eng.memset(ones_bf[:, :], 1.0).then_inc(s_pconst, 1)
            for b in range(B):
                eng.memset(hlast[b][:, :], 0.0).then_inc(s_pconst, 1)
            eng.memset(run[:, :, :], 0.0).then_inc(s_pconst, 1)
            eng.memset(farf, FAR).then_inc(s_far, 1)
            eng.wait_ge(s_pconst, 7)

            own = {"base": 0, "n": 0}

            def rstd(which, count):
                eng.wait_ge(s_var[which], count)
                wait(eng, (s_xn, s_xn2)[which], count - 1)
                eng.tensor_tensor(ve[which][:, :], mv[which][:, :, 1], eps[:, 0:TI], ALU.add)
                eng.tensor_tensor(nm[which][:, :], zero[:, 0:1].to_broadcast([P, TI]), mv[which][:, :, 0],
                                  ALU.subtract).then_inc(s_eps, 1)
                own["n"] += 1
                eng.wait_ge(s_eps, own["base"] + own["n"])
                eng.tensor_tensor(rs[which][:, :], ve[which][:, :], mhalf[:, :], ALU.pow)\
                   .then_inc(s_eps, 1)
                own["n"] += 1
                eng.wait_ge(s_eps, own["base"] + own["n"])
                eng.tensor_tensor(nm[which][:, :], nm[which][:, :], rs[which][:, :], ALU.mult)\
                   .then_inc(s_rs[which], 1)

            def start_ahead():
                eng.wait_ge(s_varx, 1)
                eng.tensor_tensor(vex[:, :], mvx[:, :, 1], eps[:, :], ALU.add)
                eng.tensor_tensor(nmx[:, :], zero[:, 0:1].to_broadcast([P, AH]), mvx[:, :, 0],
                                  ALU.subtract).then_inc(s_eps, 1)
                own["n"] += 1

            def rstd_ahead(q):
                tiles = slice((q - 1) * TI, q * TI)
                eng.wait_ge(s_eps, own["base"] + own["n"])
                eng.tensor_tensor(rnx[:, q - 1, 0:TI], vex[:, tiles], mhalf[:, :], ALU.pow)\
                   .then_inc(s_eps, 1)
                own["n"] += 1
                eng.wait_ge(s_eps, own["base"] + own["n"])
                eng.tensor_tensor(rnx[:, q - 1, TI:2 * TI], nmx[:, tiles], rnx[:, q - 1, 0:TI], ALU.mult)\
                   .then_inc(s_rsx, 1)

            def copy_rn(q, b):
                if isinstance(q, int) and q == 0:
                    eng.wait_ge(s_rsx, 1)
                else:
                    eng.wait_ge(s_rsx, NQ - 1)
                    wait_alone(eng, s_xn, q, s_rsx)
                eng.tensor_copy(rn[1 - b][:, :], rnx[:, :, :].rearrange("p q i -> p (q i)")
                                [:, bass.ds(q * 2 * TI, 2 * TI)]).then_inc(s_rn, 1)

            def left(b, which, q1):
                eng.wait_ge(s_part, 3 * q1 + which + 1)
                if which == 0:
                    eng.tensor_tensor(rest, bc32, bc3[b][:, :], ALU.subtract).then_inc(s_rest, 1)
                else:
                    eng.tensor_tensor(rest[0:64, :], rest[0:64, :], bc3[b][0:64, :], ALU.subtract)\
                       .then_inc(s_rest, 1)

            def dt_add(b, q1, h):
                eng.wait_ge(s_pm, KD * q1 + h + 1)
                part = slice(h * TC, (h + 1) * TC)
                eng.tensor_tensor(dts[b][:, part], dts[b][:, part], mag[:, part], ALU.add).then_inc(s_dt, 1)

            def v(q, b, n):
                if n >= N:
                    q, b, n = q + 1, 1 - b, n - N
                eng.wait_ge(s_Bsb, N * q + n + 1)
                wait(eng, s_b, KD * (N * q + n - 1))
                eng.tensor_tensor(pair(1, n).rearrange("p (h t) -> p h t", h=KD),
                                  xnTs[b][:, :].rearrange("p (h t) -> p h t", h=KD),
                                  Bsb[n % 4].unsqueeze(1).to_broadcast([P, KD, TC]), ALU.mult)\
                   .then_inc(s_v, 1)

            def keep_h(q, b, n):
                eng.wait_ge(s_h, ITEMS * q + KD * (n + 1))
                eng.tensor_tensor(hlast[b][:, KD * n:KD * (n + 1)],
                                  pair(2, n).rearrange("p (h t) -> p h t", h=KD)[:, :, TC - 1],
                                  zero[:, 0:1].to_broadcast([P, KD]), ALU.add).then_inc(s_hl, 1)

            def make_hc(q, n):
                h, i = KD - 1, POOLED.index(n)
                j = KD * n + h
                eng.wait_ge(s_Cs, len(POOLED) * q + i + 1)
                wait(eng, s_y, ITEMS * q + j - 3)
                eng.tensor_tensor(hc[j % 4], hb[j % 4], Csb[i % 2][:, :], ALU.mult).then_inc(s_hcp, 1)

            def enlist(q, b):
                wait_alone(eng, s_slot, q + 1, s_pconst)
                for i in range(TI):
                    eng.indirect_dma_start(
                        out=lists, out_offset=bass.IndirectOffsetOnAxis(ap=slotu[:, i:i + 1], axis=0),
                        in_=tokf[:, b * TI + i:b * TI + i + 1], in_offset=None).then_inc(s_scat, 16)

            def emit(eng, q, b, first, last):
                for n in range(N):
                    if not last or n + 2 < N:
                        v(q, b, n + 2)
                    keep_h(q, b, n)
                    if n in POOLED:
                        make_hc(q, n)
                    if first and 1 <= n < NQ:
                        rstd_ahead(n)
                    if not last:
                        if n == 1:
                            copy_rn(q, b)
                        if n == 8:
                            left(1 - b, 0, q + 1)
                        if n == 9:
                            left(1 - b, 1, q + 1)
                        if n in (13, 14):
                            dt_add(1 - b, q + 1, n - 13)
                    if not first:
                        if n == 5:
                            rstd(1, q)
                        if n == 15:
                            enlist(q - 1, 1 - b)

            rstd(0, 1)
            left(0, 0, 0)
            left(0, 1, 0)
            dt_add(0, 0, 0)
            v(0, 0, 0)
            dt_add(0, 0, 1)
            v(0, 0, 1)
            start_ahead()

            def chunk(c):
                for b in range(B):
                    q = B * c + b
                    first = isinstance(q, int) and q == 0
                    own["base"], own["n"] = 3 if first else 3 + (NQ - 1) + 2 * (q - 1), 0
                    emit(eng, q, b, first, isinstance(q, int) and q == NQ - 1)

            chunk(0)
            with eng.Fori(1, NC - 1) as c:
                chunk(c)
            chunk(NC - 1)
            own["base"], own["n"] = 3 + (NQ - 1) + 2 * (NQ - 1), 0
            rstd(1, NQ)
            enlist(NQ - 1, 1)

            def gather(t, u, r):
                c = eng.value_load(tile_cu[0:1, bass.ds(t, 1)], min_val=0, max_val=E * CAP)
                wait(eng, s_out[u], 16 * r)
                eng.tensor_copy(gcol[u][:, :], ids[:, bass.ds(c, 1)]).then_inc(s_gcol, 1)
                wait_alone(eng, s_gcol, t + 1, s_pconst)
                eng.indirect_dma_start(
                    out=mrow[u], out_offset=None, in_=token_rows,
                    in_offset=bass.IndirectOffsetOnAxis(ap=gcol[u][:, :], axis=0),
                    bounds_check=ROWS - 1, oob_is_err=False).then_inc(s_row[u], 16)

            def b1_copy(t, u):
                wait(eng, s_g, t - 3)
                e = eng.value_load(tile_eu[0:1, bass.ds(t, 1)], min_val=0, max_val=E - 1)
                eng.tensor_copy(b1c[u][:, :], sm[:, bass.ds(e * KH + OFF["b1"][0], KH)]).then_inc(s_b1, 1)

            def put(t, u):
                wait_alone(eng, s_yo, t + 1, s_pconst)
                eng.indirect_dma_start(
                    out=outrows, out_offset=bass.IndirectOffsetOnAxis(ap=gcol[u][:, :], axis=0),
                    in_=yo[u], in_offset=None,
                    bounds_check=ROWS - 1, oob_is_err=False).then_inc(s_out[u], 16)

            eng.wait_ge(s_table, 1)
            eng.wait_ge(s_store, 16 * NQ)
            for u in range(3):
                gather(u, u, 0)
            for u in range(3):
                b1_copy(u, u)

            def step(t, u, r):
                if not (isinstance(t, int) and t + 3 >= MT):
                    gather(t + 3, (u + 3) % 4, r + (u + 3) // 4)
                    b1_copy(t + 3, (u + 3) % 4)
                put(t, u)

            expert_tiles(eng, step)
            for u in range(4):
                eng.wait_ge(s_out[u], 16 * ((MT - u + 3) // 4))

        @block.scalar
        def _(eng):
            eng.preload_act_table_set("natural_log_exp_and_others")
            eng.wait_ge(s_small, 16)
            eng.activation(negA[:, :], col("logA"), ACT.Exp).then_inc(s_Ae, 1)

            def evac(q, b, name, base, place, source=misc):
                eng.wait_ge(s_full, base + place + 1)
                if name in ("xn0", "xn1"):
                    h = int(name[-1])
                    wait(eng, s_z, KD * (q - 1))
                    wait(eng, s_v, N * (q - 1))
                    eng.activation(xnT[b][h], source[:, :], ACT.Copy).then_inc(s_free, 1)
                elif name == "bc":
                    eng.activation(bc32, source[0:96, :], ACT.Copy).then_inc(s_free, 1)
                elif name == "dt1":
                    eng.activation(t1[:, :], source[0:R, :], ACT.Copy).then_inc(s_free, 1)
                elif name in ("dt2_0", "dt2_1"):
                    h = int(name[-1])
                    part = slice(h * TC, (h + 1) * TC)
                    eng.activation(dts[b][:, part], source[:, :], ACT.Relu, bias=col("bdt2", h, h + 1))
                    eng.activation(mag[:, part], source[:, :], ACT.Abs, bias=col("bdt2", h, h + 1))\
                       .then_inc(s_free, 1)
                elif name in ("z01", "z23"):
                    k = 2 if name == "z23" else 0
                    eng.activation(row[:, k:k + 2, D:2 * D], source[:, :].rearrange("p (i d) -> p i d", i=2),
                                   ACT.Copy).then_inc(s_free, 1)
                elif name in ("xnr0", "xnr1"):
                    h = int(name[-1])
                    eng.activation(xnrT[h], source[:, :], ACT.Copy).then_inc(s_free, 1)

            def part0(q, b, count):
                eng.wait_ge(s_free, count)
                wait(eng, s_C, N * (q - 1))
                eng.activation(bc3[b][:, :], bc32, ACT.Copy).then_inc(s_part, 1)

            def parts(q, b, which):
                eng.wait_ge(s_rest, 2 * q + which)
                rows = (64, 32)[which - 1]
                eng.activation(bc3[b][0:rows, :], rest[0:rows, :], ACT.Copy).then_inc(s_part, 1)

            def copy_z(q, h):
                eng.wait_ge(s_y, ITEMS * q + ITEMS - 1 + h)
                eng.activation(z[h][:, :], Y[h], ACT.Copy).then_inc(s_z, 1)

            def soft_exp(q, h, count):
                part = slice(h * TC, (h + 1) * TC)
                eng.wait_ge(s_free, count)
                eng.activation(mag[:, part], mag[:, part], ACT.Exp, scale=-1.0).then_inc(s_pms, 1)

            def soft_log(q, h):
                part = slice(h * TC, (h + 1) * TC)
                eng.wait_ge(s_pms, KD * q + h + 1)
                eng.activation(mag[:, part], mag[:, part], ACT.Ln, bias=1.0).then_inc(s_pm, 1)

            def norm1(q, tiles, rs, nm):
                for i in tiles:
                    ins = eng.activation(xin[:, i, :], xin[:, i, :], ACT.Identity,
                                         scale=rs[:, i:i + 1], bias=nm[:, i:i + 1])
                if TI - 1 in tiles:
                    ins.then_inc(s_xn, 1)

            def norm2(q, tiles):
                if 0 in tiles:
                    eng.wait_ge(s_rs[1], q + 1)
                for i in tiles:
                    ins = eng.activation(row[:, i, 0:D], row[:, i, D:2 * D], ACT.Identity,
                                         scale=rs[1][:, i:i + 1], bias=nm[1][:, i:i + 1])
                if TI - 1 in tiles:
                    ins.then_inc(s_xn2, 1)

            def copy_B(q, b, n):
                if n >= N:
                    q, b, n = q + 1, 1 - b, n - N
                M = N * q + n
                eng.wait_ge(s_Bps, M + 1)
                wait(eng, s_v, M - 3)
                eng.activation(Bsb[n % 4], Bps[:, :], ACT.Copy).then_inc(s_Bsb, 1)

            def copy_C(q, n):
                h, i = KD - 1, POOLED.index(n)
                eng.wait_ge(s_C, N * q + n + 1)
                wait(eng, s_hcp, len(POOLED) * q + i - 1)
                eng.activation(Csb[i % 2][:, :], Cps[n % 2], ACT.Copy, scale=invA[:, h * N + n:h * N + n + 1])\
                   .then_inc(s_Cs, 1)

            def exp_a(q, b, j):
                if j >= ITEMS:
                    q, b, j = q + 1, 1 - b, j - ITEMS
                n, h = divmod(j, KD)
                if n == 0:
                    eng.wait_ge(s_dt, KD * q + h + 1)
                wait(eng, s_h, ITEMS * q + j - 1)
                eng.activation(A[j % 2][:, :], dts[b][:, h * TC:(h + 1) * TC], ACT.Exp,
                               scale=negA[:, h * N + n:h * N + n + 1]).then_inc(s_a, 1)

            def emit(eng, q, b, first, last):
                at, order = hops(first, last)
                base = hop_base(q)
                for n in range(N):
                    exp_a(q, b, 2 * n + 1)
                    if n in POOLED:
                        copy_C(q, n)
                    name, place = at.get(n - 1, ("", 0))
                    if name in PRE:
                        evac(q + 1, 1 - b, name, base, place)
                    elif name in ("z01", "z23", "xnr0", "xnr1"):
                        evac(q - 1, 1 - b, name, base, place)
                    if not first and n == 1:
                        for h in range(KD):
                            copy_z(q - 1, h)
                    if not last or n + 1 < N:
                        exp_a(q, b, 2 * n + 2)
                    if not last or n + 3 < N:
                        copy_B(q, b, n + 3)
                    if not last:
                        if n == 7:
                            part0(q + 1, 1 - b, base + order["bc"] + 1)
                        if n == 9:
                            parts(q + 1, 1 - b, 1)
                        if n == 10:
                            parts(q + 1, 1 - b, 2)
                        m = n - 2
                        if m in (0, 1):
                            if m == 0:
                                eng.wait_ge(s_x, 16 * (q + 2))
                                eng.wait_ge(s_rn, q + 1)
                            norm1(q + 1, (2 * m, 2 * m + 1), rn[1 - b][:, 0:TI], rn[1 - b][:, TI:2 * TI])
                        if n in (12, 13):
                            soft_exp(q + 1, n - 12, base + order[f"dt2_{n - 12}"] + 1)
                        if n in (13, 14):
                            soft_log(q + 1, n - 13)
                    if first and n == 4:
                        load_weights()
                    if not first and n in (6, 7):
                        norm2(q - 1, (2 * (n - 6), 2 * (n - 6) + 1))
                    if not first and n == 11:
                        softmax_exp(q - 1)

            def load_weights():
                eng.dma_start(b2_sb[:, :], b2).then_inc(s_b2, 16)
                eng.wait_ge(s_varx, 1)
                for k in range(KD):
                    eng.dma_start(w1_sb[:, k, :], w1[:, k, :]).then_inc(s_w, 16)
                eng.dma_start(w2_sb[:, 0:ring_at], w2[:, 0:ring_at]).then_inc(s_w2a, 16)

            def softmax_exp(q):
                eng.wait_ge(s_lg, q + 1)
                eng.activation(lg[:, :, :], lg[:, :, :], ACT.Exp).then_inc(s_pe, 1)

            eng.wait_ge(s_rs[0], 1)
            norm1(0, range(TI), rs[0], nm[0])
            for i, name in enumerate(PRE):
                evac(0, 0, name, 0, i, start_bank[name])
                if name == "bc":
                    part0(0, 0, i + 1)
                    parts(0, 0, 1)
                if name == "dt1":
                    parts(0, 0, 2)
                if name in ("dt2_0", "dt2_1"):
                    soft_exp(0, int(name[-1]), i + 1)
                    soft_log(0, int(name[-1]))
                if name == "dt2_0":
                    copy_B(0, 0, 0)
            eng.wait_ge(s_const, 4 + KD)
            exp_a(0, 0, 0)
            copy_B(0, 0, 1)
            copy_B(0, 0, 2)
            phases(emit)(eng)
            for h in range(KD):
                copy_z(NQ - 1, h)
            for i, name in enumerate(("z01", "z23", "xnr0", "xnr1")):
                if name == "xnr0":
                    norm2(NQ - 1, range(TI))
                evac(NQ - 1, 1, name, LAST_BASE, i, last_bank[name])
            softmax_exp(NQ - 1)

            eng.preload_act_table_set("gelu_and_others")

            def gelus(t, u):
                eng.wait_ge(s_b1, t + 1)
                wait(eng, s_yp, t - 1)
                for j in range(KH):
                    if j % 4 == 0:
                        eng.wait_ge(s_hps, 2 * t + j // 4 + 1)
                    g = eng.activation(hT[u % 2][:, j * P:(j + 1) * P], hps[u % 2][:, j * P:(j + 1) * P],
                                       ACT.Gelu, bias=b1c[u][:, j:j + 1])
                g.then_inc(s_g, 1)

            def step(t, u, r):
                gelus(t, u)

            expert_tiles(eng, step)

        @block.tensor
        def _(eng):
            def fill(q, b, name, base, place, to=misc, free=None):
                wait(eng, s_free, base + (place if free is None else free))
                if name in ("xn0", "xn1"):
                    h = int(name[-1])
                    eng.wait_ge(s_xn, q + 1)
                    for i in range(TI):
                        mm = eng.transpose(to[:, i * P:(i + 1) * P], xin[:, i, h * P:(h + 1) * P], ident)
                elif name == "bc":
                    for h in range(KD):
                        mm = eng.matmul(to[0:96, :], col("wbc", h * 96, h * 96 + 96), xnT[b][h],
                                        start=(h == 0), stop=(h == KD - 1))
                elif name == "dt1":
                    for h in range(KD):
                        mm = eng.matmul(to[0:R, :], col("wdt1", h * R, h * R + R), xnT[b][h],
                                        start=(h == 0), stop=(h == KD - 1))
                elif name in ("dt2_0", "dt2_1"):
                    h = int(name[-1])
                    lo = OFF["wdt2"][0]
                    mm = eng.matmul(to[:, :], sm[0:R, lo + h * P:lo + (h + 1) * P], t1[:, :],
                                    start=True, stop=True)
                elif name in ("z01", "z23"):
                    eng.wait_ge(s_z, KD * q + KD)
                    eng.wait_ge(s_res, 16 * (q + 1))
                    for i in range(2):
                        k = i + (2 if name == "z23" else 0)
                        eng.matmul(to[:, i * D:(i + 1) * D], ident, row[:, k, D:2 * D],
                                   start=True, stop=False)
                        for h in range(KD):
                            mm = eng.matmul(to[:, (i * KD + h) * P:(i * KD + h + 1) * P],
                                            z[h][:, k * P:(k + 1) * P], ident, start=False,
                                            stop=(h == KD - 1))
                elif name in ("xnr0", "xnr1"):
                    h = int(name[-1])
                    eng.wait_ge(s_xn2, q + 1)
                    for i in range(TI):
                        mm = eng.transpose(to[:, i * P:(i + 1) * P], row[:, i, h * P:(h + 1) * P], ident)
                elif name == "route":
                    for i in range(TI):
                        for h in range(KD):
                            mm = eng.matmul(to[:, i * E:(i + 1) * E], xnrT[h][:, i * P:(i + 1) * P],
                                            col("wr", h * E, (h + 1) * E), start=(h == 0), stop=(h == KD - 1))
                elif name == "rank":
                    eng.wait_ge(s_oh, q + 1)
                    eng.matmul(to[:, 0:TI * E], tri_bf[:, :], onehot[:, :, :].rearrange("p i e -> p (i e)"),
                               start=True, stop=True)
                    mm = eng.matmul(to[:, TI * E:2 * TI * E], ones_bf[:, :],
                                    onehot[:, :, :].rearrange("p i e -> p (i e)"), start=True, stop=True)
                mm.then_inc(s_full, 1)

            def spread_B(q, b, n):
                if n >= N:
                    q, b, n = q + 1, 1 - b, n - N
                M = N * q + n
                if n == 0:
                    eng.wait_ge(s_part, 3 * q + 3)
                wait(eng, s_Bsb, M)
                eng.matmul(Bps[:, :], sel[:, n, :], bc3[b][:, :], start=True, stop=True).then_inc(s_Bps, 1)

            def spread_C(q, b, n):
                if n >= N:
                    q, b, n = q + 1, 1 - b, n - N
                M = N * q + n
                if n < 2:
                    q0, m = q - 1, n + N - 2
                else:
                    q0, m = q, n - 2
                if not (isinstance(M, int) and M < 2):
                    h = 0 if m in POOLED else KD - 1
                    eng.wait_ge(s_hc, VECTOR_ITEMS * q0 + made_before(KD * m + h + 1))
                    if m in POOLED:
                        eng.wait_ge(s_Cs, len(POOLED) * q0 + POOLED.index(m) + 1)
                eng.matmul(Cps[n % 2], sel[:, N + n, :], bc3[b][:, :], start=True, stop=True)\
                   .then_inc(s_C, 1)

            def add_y(q, j):
                if j < 0:
                    q, j = q - 1, j + ITEMS
                n, h = divmod(j, KD)
                if pooled(n, h):
                    eng.wait_ge(s_hcp, len(POOLED) * q + POOLED.index(n) + 1)
                else:
                    eng.wait_ge(s_hc, VECTOR_ITEMS * q + made_before(j + 1))
                eng.matmul(Y[h], ident, hc[j % 4], start=False, stop=(n == N - 1)).then_inc(s_y, 1)

            def start_y(q, b):
                for h in range(KD):
                    wait(eng, s_z, KD * (q - 1) + h + 1)
                    eng.matmul(Y[h], dskip[:, h, :], xnT[b][h], start=True, stop=False)

            def emit(eng, q, b, first, last):
                at, order = hops(first, last)
                base = hop_base(q)
                for n in range(N):
                    if not last or n + 3 < N:
                        spread_B(q, b, n + 3)
                    if not last or n + 1 < N:
                        spread_C(q, b, n + 1)
                    if n in at:
                        name, place = at[n]
                        if name in PRE:
                            fill(q + 1, 1 - b, name, base, place)
                        else:
                            fill(q - 1, 1 - b, name, base, place)
                    if n == 1:
                        start_y(q, b)
                    if n > 0 or not first:
                        add_y(q, 2 * n - 2)
                        add_y(q, 2 * n - 1)

            def keep_busy(times, fixed, moving):
                for _ in range(times):
                    eng.matmul(bank[1][:, 0:moving.shape[1]], fixed, moving, start=True, stop=True)

            eng.wait_ge(s_small, 16)
            for i, name in enumerate(PRE):
                fill(0, 0, name, 0, i, start_bank[name], i - i % 2)
                if name == "dt2_0":
                    eng.wait_ge(s_const, 4 + KD)
                    spread_B(0, 0, 0)
            spread_C(0, 0, 0)
            spread_B(0, 0, 1)
            spread_B(0, 0, 2)
            eng.wait_ge(s_free, len(PRE))
            phases(emit)(eng)
            add_y(NQ, -2)
            add_y(NQ, -1)
            for i, name in enumerate(POST):
                fill(NQ - 1, 1, name, LAST_BASE, i, last_bank[name], i - (name in ("z23", "xnr1")))
            eng.wait_ge(s_lists, 16)
            eng.wait_ge(s_slot, NQ)
            for i in range(E * CAP // P):
                mm = eng.transpose(misc[:, i * P:(i + 1) * P], lists_in[:, i * P:(i + 1) * P], ident)
            mm.then_inc(s_lt, 1)

            def turn_x(t, u, r):
                eng.wait_ge(s_row[u], 16 * (r + 1))
                wait(eng, s_xT, t - 1)
                for h in range(KD):
                    mm = eng.transpose(xTps[u % 2][:, h * P:(h + 1) * P], mrow[u][:, h * P:(h + 1) * P],
                                       ident)
                mm.then_inc(s_xTp, 1)

            def hidden(t, u):
                eng.wait_ge(s_w1c, t + 1)
                eng.wait_ge(s_xT, t + 1)
                wait(eng, s_g, t - 1)
                for j in range(KH):
                    for h in range(KD):
                        mm = eng.matmul(hps[u % 2][:, j * P:(j + 1) * P], w1c[u % 2][h][:, j * P:(j + 1) * P],
                                        xT[u % 2][:, h * P:(h + 1) * P],
                                        start=(h == 0), stop=(h == KD - 1))
                    if j % 4 == 3:
                        mm.then_inc(s_hps, 1)

            def outputs(t, u):
                e = eng.value_load(tile_eu[0:1, bass.ds(t, 1)], min_val=0, max_val=E - 1)
                eng.wait_ge(s_g, t + 1)
                wait(eng, s_ys, t - 1)
                for j in range(KH):
                    mm = eng.matmul(yps[u % 2][:, 0:D], hT[u % 2][:, j * P:(j + 1) * P],
                                    w2_sb[:, bass.ds(e * KH * D + j * D, D)],
                                    start=(j == 0), stop=(j == KH - 1))
                mm.then_inc(s_yp, 1)

            keep_busy(12, ones_bf[0:96, :], sel[:, 0:4, :].rearrange("k m p -> k (m p)"))
            eng.wait_ge(s_table, 1)
            turn_x(0, 0, 0)
            hidden(0, 0)
            turn_x(1, 1, 0)
            eng.wait_ge(s_w2a, 16)
            eng.wait_ge(s_w2b, 16)

            def step(t, u, r):
                if not (isinstance(t, int) and t + 1 >= MT):
                    hidden(t + 1, (u + 1) % 4)
                if not (isinstance(t, int) and t + 2 >= MT):
                    turn_x(t + 2, (u + 2) % 4, r + (u + 2) // 4)
                outputs(t, u)

            expert_tiles(eng, step)

        @block.vector
        def _(eng):
            own = {"ln": 0, "rt": 0, "tab": 0}
            sems = {"ln": s_ln, "rt": s_rt, "tab": s_tab}
            bases = {"ln": 0, "rt": 0, "tab": 0}

            def signal(ins, kind):
                ins.then_inc(sems[kind], 1)
                own[kind] += 1

            def settle(kind):
                eng.wait_ge(sems[kind], bases[kind] + own[kind])

            def done(ins, kind):
                ins.then_inc(sems[kind], 1)
                own[kind] += 1
                eng.wait_ge(sems[kind], bases[kind] + own[kind])

            def stats(which, i, src):
                eng.bn_stats(st[which][:, i * 6:(i + 1) * 6], src).then_inc(s_ln, 1)
                own["ln"] += 1

            def aggregate(which, count):
                wait(eng, (s_xn, s_xn2)[which], count)
                wait_alone(eng, s_ln, bases["ln"] + own["ln"], s_x)
                for i in range(TI):
                    ins = eng.bn_aggr(mv[which][:, i, :], st[which][:, i * 6:(i + 1) * 6])
                ins.then_inc(s_var[which], 1)

            def ln1_stats(q, tiles):
                eng.wait_ge(s_x, 16 * (q + 1))
                for i in tiles:
                    stats(0, i, xin[:, i, :])

            ln1_stats(0, range(TI))
            aggregate(0, 0)
            eng.wait_ge(s_small, 16)
            eng.wait_ge(s_Ae, 1)
            done(eng.tensor_scalar(negA[:, :], negA[:, :], -1.0, None, ALU.mult), "tab")
            done(eng.tensor_scalar(invA[:, :], negA[:, :], 1e-8, None, ALU.add), "tab")
            eng.reciprocal(invA[:, :], invA[:, :]).then_inc(s_const, 1)
            eng.tensor_copy(sel[:, :, :], sm[0:96, OFF["spread"][0]:OFF["spread"][1]].unsqueeze(2)
                            .to_broadcast([96, 32, P])).then_inc(s_const, 1)
            eng.tensor_copy(tri_bf[:, :], col("tri")).then_inc(s_const, 1)
            eng.tensor_copy(tokf[:, :], col("tok0")).then_inc(s_const, 1)
            for h in range(KD):
                eng.tensor_scalar(dskip[:, h, :], ident, col("dskip", h, h + 1), None, ALU.mult)\
                   .then_inc(s_const, 1)

            def make_b(q, b, j):
                if j >= ITEMS:
                    q, b, j = q + 1, 1 - b, j - ITEMS
                n, h = divmod(j, KD)
                eng.wait_ge(s_a, ITEMS * q + j + 1)
                if h == 0:
                    eng.wait_ge(s_v, N * q + n + 1)
                eng.scalar_tensor_tensor(bb[j % 2][:, :], A[j % 2][:, :], 1.0, vb[j % 4],
                                         ALU.subtract, ALU.mult).then_inc(s_b, 1)

            def scan(q, b, j):
                n, h = divmod(j, KD)
                eng.wait_ge(s_b, ITEMS * q + j + 1)
                if h == 0:
                    wait(eng, s_hl, N * q + n - 1)
                elif n - 2 in POOLED:
                    eng.wait_ge(s_hcp, len(POOLED) * q + POOLED.index(n - 2) + 1)
                eng.tensor_tensor_scan(hb[j % 4], A[j % 2][:, :], bb[j % 2][:, :], hlast[b][:, j:j + 1],
                                       ALU.mult, ALU.add).then_inc(s_h, 1)

            def make_hc(q, b, j):
                if j < 0:
                    q, b, j = q - 1, 1 - b, j + ITEMS
                n, h = divmod(j, KD)
                if pooled(n, h):
                    return
                eng.wait_ge(s_h, ITEMS * q + j + 1)
                if h == 0:
                    eng.wait_ge(s_C, N * q + n + 1)
                    wait(eng, s_y, KD * (N * q + n - 1))
                eng.scalar_tensor_tensor(hc[j % 4], hb[j % 4], invA[:, h * N + n:h * N + n + 1],
                                         Cps[n % 2], ALU.mult, ALU.mult).then_inc(s_hc, 1)

            def ln2_stats(which, base, place):
                eng.wait_ge(s_free, base + place + 1)
                for i in range(2 * which, 2 * which + 2):
                    stats(1, i, row[:, i, D:2 * D])

            def over_e(ap):
                return ap.unsqueeze(2).to_broadcast([P, TI, E])

            less8 = col("e_less8").unsqueeze(1).to_broadcast([P, TI, E])

            def logits(q, base, place, k):
                if k == 0:
                    eng.wait_ge(s_full, base + place + 1)
                    eng.tensor_tensor(lg[:, :, :], misc[:, 0:TI * E].rearrange("p (i e) -> p i e", e=E),
                                      col("br").unsqueeze(1).to_broadcast([P, TI, E]), ALU.add)\
                       .then_inc(s_free, 1)
                elif k == 1:
                    eng.wait_ge(s_free, base + place + 1)
                    signal(eng.tensor_reduce(red[:, :], lg[:, :, :], AX.X, ALU.max), "rt")
                else:
                    settle("rt")
                    eng.tensor_tensor(lg[:, :, :], lg[:, :, :], over_e(red[:, :]), ALU.subtract)\
                       .then_inc(s_lg, 1)

            def choose(q, k):
                if k == 0:
                    eng.wait_ge(s_pe, q + 1)
                    signal(eng.tensor_reduce(red[:, :], lg[:, :, :], AX.X, ALU.add), "rt")
                    return
                settle("rt")
                if k == 1:
                    signal(eng.reciprocal(red[:, :], red[:, :]), "rt")
                elif k == 2:
                    signal(eng.tensor_tensor(lg[:, :, :], lg[:, :, :], over_e(red[:, :]), ALU.mult), "rt")
                elif k == 3:
                    signal(eng.tensor_reduce(red[:, :], lg[:, :, :], AX.X, ALU.max), "rt")
                elif k == 4:
                    signal(eng.tensor_tensor(lg[:, :, :], lg[:, :, :], over_e(red[:, :]), ALU.is_equal),
                           "rt")
                elif k == 5:
                    signal(eng.tensor_tensor(lg[:, :, :], lg[:, :, :], less8, ALU.mult), "rt")
                elif k == 6:
                    signal(eng.tensor_reduce(pick[:, :], lg[:, :, :], AX.X, ALU.min), "rt")
                else:
                    eng.tensor_tensor(onehot[:, :, :], over_e(pick[:, :]), less8, ALU.is_equal)\
                       .then_inc(s_oh, 1)

            def place_tokens(q, b, base, place, k):
                if k == 0:
                    eng.wait_ge(s_full, base + place + 1)
                    signal(eng.tensor_copy(run[:, 0, :], run[:, TI, :]), "rt")
                elif k <= TI:
                    settle("rt")
                    signal(eng.tensor_tensor(run[:, k, :], run[:, k - 1, :],
                                             misc[:, (TI + k - 1) * E:(TI + k) * E], ALU.add), "rt")
                elif k == TI + 1:
                    settle("rt")
                    eng.tensor_tensor(slot[:, :, :], misc[:, 0:TI * E].rearrange("p (i e) -> p i e", e=E),
                                      run[:, 0:TI, :], ALU.add).then_inc(s_free, 1)
                elif k == TI + 2:
                    eng.wait_ge(s_free, base + place + 1)
                    signal(eng.tensor_tensor(slot[:, :, :], slot[:, :, :], onehot[:, :, :], ALU.mult), "rt")
                elif k == TI + 3:
                    settle("rt")
                    signal(eng.tensor_reduce(slotf[:, :], slot[:, :, :], AX.X, ALU.add), "rt")
                else:
                    wait(eng, s_scat, 16 * TI * q)
                    eng.tensor_scalar(tokf[:, b * TI:(b + 1) * TI], tokf[:, b * TI:(b + 1) * TI],
                                      float(TC), None, ALU.add)
                    settle("rt")
                    eng.tensor_copy(slotu[:, :], slotf[:, :]).then_inc(s_slot, 1)

            def emit(eng, q, b, first, last):
                at, order = hops(first, last)
                base = hop_base(q)
                bases["ln"], own["ln"] = NQ * TI if first else NQ * TI + TI * (q - 1), 0
                bases["rt"], own["rt"] = RT_STEPS * (q - 1), 0

                def between(j, gap):
                    if not first:
                        if j == 7 and gap == 1:
                            ln2_stats(0, base, order["z01"])
                        if j == 9 and gap == 1:
                            ln2_stats(1, base, order["z23"])
                        if j == 10 and gap == 0:
                            aggregate(1, q - 1)
                        if (j, gap) in ((21, 1), (22, 0), (22, 1)):
                            logits(q - 1, base, order["route"], 2 * (j - 21) + gap - 1)
                        if 24 <= j < 28:
                            choose(q - 1, 2 * (j - 24) + gap)
                        if (j, gap) >= (29, 1):
                            k = 2 * (j - 29) + gap - 1
                            for step in range(k, 9 if k == 4 else k + 1):
                                place_tokens(q - 1, 1 - b, base, order["rank"], step)

                for j in range(ITEMS):
                    scan(q, b, j)
                    if not last or j + 1 < ITEMS:
                        make_b(q, b, j + 1)
                    between(j, 0)
                    if not (first and j == 0):
                        make_hc(q, b, j - 1)
                    between(j, 1)

            for q in range(1, NQ):
                eng.wait_ge(s_ahead[q - 1], 16)
                for i in range(TI):
                    k = (q - 1) * TI + i
                    eng.bn_stats(stx[:, k * 6:(k + 1) * 6], x_ahead(q)[:, i, :]).then_inc(s_ln, 1)
                    own["ln"] += 1
            assert own["ln"] == NQ * TI
            eng.wait_ge(s_ln, NQ * TI)
            for k in range(AH):
                ins = eng.bn_aggr(mvx[:, k, :], stx[:, k * 6:(k + 1) * 6])
            ins.then_inc(s_varx, 1)
            eng.wait_ge(s_pconst, 7)
            eng.tensor_copy(run[:, TI, :], col("e_base")).then_inc(s_const, 1)
            eng.wait_ge(s_init, 16)
            eng.wait_ge(s_const, 5 + KD)
            make_b(0, 0, 0)
            phases(emit)(eng)
            make_hc(NQ, 0, -1)
            bases["ln"], own["ln"] = NQ * TI + TI * (NQ - 1), 0
            bases["rt"], own["rt"] = RT_STEPS * (NQ - 1), 0
            q = NQ - 1
            for i in range(2):
                ln2_stats(i, LAST_BASE, i)
            aggregate(1, q)
            for k in range(3):
                logits(q, LAST_BASE, 4, k)
            for k in range(8):
                choose(q, k)
            for k in range(9):
                place_tokens(q, 1, LAST_BASE, 5, k)

            cnt = ntok[:, :]
            done(eng.tensor_tensor(cnt, run[:, TI, :], col("e_base"), ALU.subtract), "tab")
            g1 = big[:, 0:E * 32].rearrange("p (e j) -> p e j", j=32)
            done(eng.tensor_tensor(g1, cnt.unsqueeze(2).to_broadcast([P, E, 32]),
                                   col("j128").unsqueeze(1).to_broadcast([P, E, 32]), ALU.is_gt), "tab")
            done(eng.tensor_reduce(ntile[:, :], g1, AX.X, ALU.add), "tab")
            done(eng.memset(cum[:, 0:1], 0.0), "tab")
            for e in range(E):
                done(eng.tensor_tensor(cum[:, e + 1:e + 2], cum[:, e:e + 1], ntile[:, e:e + 1], ALU.add),
                     "tab")
            g2 = big[:, 0:MT * E].rearrange("p (k e) -> p k e", e=E)
            g3 = big2[:, 0:MT * E].rearrange("p (k e) -> p k e", e=E)
            no = col("tile_no").unsqueeze(2).to_broadcast([P, MT, E])

            def over_k(ap):
                return ap.unsqueeze(1).to_broadcast([P, MT, E])

            done(eng.tensor_tensor(g2, over_k(cum[:, 1:E + 1]), no, ALU.is_le), "tab")
            done(eng.tensor_reduce(tile_e[:, :], g2, AX.X, ALU.add), "tab")
            done(eng.tensor_tensor(g3, g2, over_k(ntile[:, :]), ALU.mult), "tab")
            done(eng.tensor_reduce(tile_c[:, :], g3, AX.X, ALU.add), "tab")
            done(eng.tensor_tensor(tile_c[:, :], col("tile_no"), tile_c[:, :], ALU.subtract), "tab")
            done(eng.scalar_tensor_tensor(tile_c[:, :], tile_e[:, :], float(CAP), tile_c[:, :],
                                          ALU.mult, ALU.add), "tab")
            done(eng.tensor_scalar(tile_cu[:, :], tile_c[:, :], float(E * CAP), None, ALU.min), "tab")
            done(eng.tensor_scalar(tile_eu[:, :], tile_e[:, :], float(E - 1), None, ALU.min), "tab")
            done(eng.memset(red[:, 0:1], FAR), "tab")
            done(eng.tensor_copy(ids[:, E * CAP:E * CAP + 1], red[:, 0:1]), "tab")
            eng.wait_ge(s_lt, 1)
            eng.tensor_copy(ids[:, 0:E * CAP], misc[:, 0:E * CAP]).then_inc(s_table, 1)

            def copy_W1(t, u):
                wait(eng, s_hps, 2 * t - 2)
                e = eng.value_load(tile_eu[0:1, bass.ds(t, 1)], min_val=0, max_val=E - 1)
                for h in range(KD):
                    c = eng.tensor_copy(w1c[u % 2][h][:, :], w1_sb[:, h, bass.ds(e * H, H)])
                c.then_inc(s_w1c, 1)

            def copy_xT(t, u):
                eng.wait_ge(s_xTp, t + 1)
                wait(eng, s_hps, 2 * t - 2)
                eng.tensor_copy(xT[u % 2], xTps[u % 2][:, 0:D]).then_inc(s_xT, 1)

            def finish(t, u, r):
                e = eng.value_load(tile_eu[0:1, bass.ds(t, 1)], min_val=0, max_val=E - 1)
                eng.wait_ge(s_yp, t + 1)
                wait(eng, s_out[u], 16 * r)
                eng.tensor_tensor(yo[u], yps[u % 2][:, 0:D], b2_sb[:, bass.ds(e * D, D)], ALU.add)\
                   .then_inc(s_ys, 1)
                eng.wait_ge(s_ys, t + 1)
                eng.tensor_tensor(yo[u], yo[u], mrow[u][:, D:2 * D], ALU.add).then_inc(s_yo, 1)

            eng.wait_ge(s_w, 16 * KD)
            copy_W1(0, 0)
            copy_W1(1, 1)
            eng.wait_ge(s_b2, 16)
            copy_xT(0, 0)
            copy_xT(1, 1)

            def step(t, u, r):
                if not (isinstance(t, int) and t + 2 >= MT):
                    copy_W1(t + 2, (u + 2) % 4)
                    copy_xT(t + 2, (u + 2) % 4)
                finish(t, u, r)

            expert_tiles(eng, step)


def kernel(**inputs):
    import concourse.bacc as bacc
    from concourse.bass_utils import run_bass_kernel_spmd

    a = {k.removeprefix("L0_"): np.asarray(v) for k, v in inputs.items()}

    def halves(w):
        return w.reshape(KD, P, -1).transpose(1, 0, 2).reshape(P, -1)

    def pad(w):
        return np.concatenate([w, np.zeros((P - w.shape[0], w.shape[1]), np.float32)])

    f = np.float32
    one = np.arange(P)
    bc = np.concatenate([a["attn_W_B"], a["attn_W_C"]]).T
    parts = dict(
        ident=np.eye(P, dtype=f), logA=halves(a["attn_log_A"]), bdt2=halves(a["attn_b_dt2"][:, None]),
        dskip=halves(a["attn_D_skip"][:, None]), wr=halves(a["ffn_Wr"]),
        wbc=halves(np.concatenate([bc, bc, bc], axis=1)), wdt1=halves(a["attn_W_dt1"].T),
        wdt2=pad(a["attn_W_dt2"].T),
        b1=a["ffn_b1"].reshape(E, KH, P).transpose(2, 0, 1).reshape(P, -1),
        tri=(one[:, None] < one[None, :]).astype(f),
        spread=pad((np.arange(96)[:, None] % 32 == np.arange(32)[None, :]).astype(f)),
        e_less8=np.tile(np.arange(E, dtype=f) - E, (P, 1)),
        e_base=np.tile(np.arange(E, dtype=f) * ROWS, (P, 1)),
        tok0=(np.arange(B)[None, :, None] * T + np.arange(TI)[None, None, :] * P - TC
              + one[:, None, None]).reshape(P, -1).astype(f),
        j128=np.tile(np.arange(32, dtype=f) * P, (P, 1)),
        tile_no=np.tile(np.arange(MT, dtype=f), (P, 1)),
        br=np.tile(a["ffn_br"], (P, 1)))
    assert list(parts) == list(SMALL)
    arrays = {
        "x_in": np.ascontiguousarray(a["attn_x"]),
        "small_in": np.ascontiguousarray(np.concatenate(list(parts.values()), axis=1)),
        "w1_in": np.ascontiguousarray(
            a["ffn_W1"].reshape(E, KD, P, H).transpose(2, 1, 0, 3).reshape(P, KD, E * H)),
        "w2_in": np.ascontiguousarray(
            a["ffn_W2"].reshape(E, KH, P, D).transpose(2, 0, 1, 3).reshape(P, E * KH * D)),
        "b2_in": np.ascontiguousarray(np.tile(a["ffn_b2"].reshape(1, -1), (P, 1))),
    }
    nc = bacc.Bacc("TRN2", target_bir_lowering=False, num_devices=1)
    args = [nc.dram_tensor(n, v.shape, mybir.dt.from_np(v.dtype), kind="ExternalInput").ap()
            for n, v in arrays.items()]
    out = nc.dram_tensor("y_out", (B, T, D), F32, kind="ExternalOutput").ap()
    build(nc, *args, out)
    r = run_bass_kernel_spmd(nc, [arrays], core_ids=[0])
    return r.results[0]["y_out"]
```
